# Optimizing a Trainium2 kernel written in Bass

```python
import numpy as np
import jax
import jax.numpy as jnp

def _softmax(x, axis=-1):
    return jax.nn.softmax(x, axis=axis)

def _gelu(x):
    return jax.nn.gelu(x, approximate=True)

def _silu(x):
    return jax.nn.silu(x)

def _sigmoid(x):
    return jax.nn.sigmoid(x)

def _layernorm(x, axis=-1, eps=1e-05):
    m = jnp.mean(x, axis=axis, keepdims=True)
    v = jnp.var(x, axis=axis, keepdims=True)
    return (x - m) / jnp.sqrt(v + eps)

def _scatter_add(tgt, idx, src, axis=0):
    return tgt.at[idx].add(src)

def _segment_sum(src, seg, n):
    return jax.ops.segment_sum(src, seg, n)
kernel_name = 'mk_gnn_preln_d2_gnn_r64_f05326'

def setup_inputs(seed: int=0):
    np.random.seed(seed)
    _w = jnp.asarray

    def _rec_inputs():
        import jax
        import jax.numpy as jnp
        _gk = jax.random.key(seed)
        x = -0.0005121 + 1.001 * jax.random.normal(jax.random.fold_in(_gk, 1), (100000, 64), jnp.float32)
        src = jax.random.randint(jax.random.fold_in(_gk, 2), (50000,), 0, 100000, jnp.int32)
        dst = jnp.minimum((100000 * jax.random.uniform(jax.random.fold_in(_gk, 3), (50000,)) ** 2.0).astype(jnp.int32), 99999)
        _o = jnp.argsort(dst, stable=True)
        src = src[_o]
        dst = dst[_o]
        edge_attr_16 = 0.000254156 + 0.999948 * jax.random.normal(jax.random.fold_in(_gk, 11), (50000, 16), jnp.float32)
        return (x, src, dst, edge_attr_16)
    x, src, dst, edge_attr_16 = _rec_inputs()

    def _L0_gnn_setup():
        import jax, jax.numpy as jnp
        import numpy as np
        N, E = (50000, 12500)
        NODE_DIM, EDGE_DIM, HEADS = (64, 16, 4)
        C = NODE_DIM // HEADS
        NEG_SLOPE = 0.2
        BN_EPS = 1e-05
        key = jax.random.key(seed)
        ks = jax.random.split(key, 12)
        glorot = lambda k, shape: jax.random.normal(k, shape, jnp.float32) * np.sqrt(2.0 / (shape[0] + shape[-1]))
        return {'x': jax.random.normal(ks[0], (N, NODE_DIM), jnp.float32), 'edge_index': jax.random.randint(ks[1], (2, E), 0, N, jnp.int32), 'edge_attr': jax.random.normal(ks[2], (E, EDGE_DIM), jnp.float32), 'W_l': glorot(ks[3], (NODE_DIM, HEADS * C)), 'b_l': jnp.zeros((HEADS * C,), jnp.float32), 'W_r': glorot(ks[4], (NODE_DIM, HEADS * C)), 'b_r': jnp.zeros((HEADS * C,), jnp.float32), 'W_e': glorot(ks[5], (EDGE_DIM, HEADS * C)), 'att': glorot(ks[6], (HEADS, C)), 'bias': jnp.zeros((HEADS * C,), jnp.float32), 'gamma': jnp.ones((NODE_DIM,), jnp.float32), 'beta': jnp.zeros((NODE_DIM,), jnp.float32)}
    _L0_gnn_all = _L0_gnn_setup()
    _L0_gnn_in = {k: v for k, v in _L0_gnn_all.items() if k in ('W_l', 'b_l', 'W_r', 'b_r', 'W_e', 'att', 'bias', 'gamma', 'beta')}
    del _L0_gnn_all

    def _L1_gnn_setup():
        import jax, jax.numpy as jnp
        import numpy as np
        N_NODES = 50000
        N_EDGES = 12500
        D = 64
        key = jax.random.key(seed)
        k1, k2, k3 = jax.random.split(key, 3)
        x = jax.random.normal(k1, (N_NODES, D), dtype=jnp.float32)
        edge_index = jax.random.randint(k2, (2, N_EDGES), 0, N_NODES, dtype=jnp.int64)
        W = jax.random.normal(k3, (D, D), dtype=jnp.float32) * (1.0 / np.sqrt(D))
        b = jnp.zeros((D,), dtype=jnp.float32)
        return {'x': x, 'edge_index': edge_index, 'W': W, 'b': b}
    _L1_gnn_all = _L1_gnn_setup()
    _L1_gnn_in = {k: v for k, v in _L1_gnn_all.items() if k in ('W', 'b')}
    del _L1_gnn_all
    return {'x': x, 'src': src, 'dst': dst, 'edge_attr_16': edge_attr_16, 'L0_gnn_W_l': _L0_gnn_in['W_l'], 'L0_gnn_b_l': _L0_gnn_in['b_l'], 'L0_gnn_W_r': _L0_gnn_in['W_r'], 'L0_gnn_b_r': _L0_gnn_in['b_r'], 'L0_gnn_W_e': _L0_gnn_in['W_e'], 'L0_gnn_att': _L0_gnn_in['att'], 'L0_gnn_bias': _L0_gnn_in['bias'], 'L0_gnn_gamma': _L0_gnn_in['gamma'], 'L0_gnn_beta': _L0_gnn_in['beta'], 'L1_gnn_W': _L1_gnn_in['W'], 'L1_gnn_b': _L1_gnn_in['b']}

def reference(x, src, dst, edge_attr_16, L0_gnn_W_l, L0_gnn_b_l, L0_gnn_W_r, L0_gnn_b_r, L0_gnn_W_e, L0_gnn_att, L0_gnn_bias, L0_gnn_gamma, L0_gnn_beta, L1_gnn_W, L1_gnn_b):
    import jax
    import jax.numpy as jnp

    def _L0_gnn_ref(x, edge_index, edge_attr, W_l, b_l, W_r, b_r, W_e, att, bias, gamma, beta):
        import jax, jax.numpy as jnp
        import numpy as np
        N, E = (50000, 12500)
        NODE_DIM, EDGE_DIM, HEADS = (64, 16, 4)
        C = NODE_DIM // HEADS
        NEG_SLOPE = 0.2
        BN_EPS = 1e-05
        src, dst = (edge_index[0], edge_index[1])
        n = x.shape[0]
        xl = (x @ W_l + b_l).reshape(n, HEADS, C)
        xr = (x @ W_r + b_r).reshape(n, HEADS, C)
        e = (edge_attr @ W_e).reshape(-1, HEADS, C)
        g = jax.nn.leaky_relu(xl[src] + xr[dst] + e, NEG_SLOPE)
        logits = jnp.einsum('ehc,hc->eh', g, att)
        amax = jax.ops.segment_max(logits, dst, num_segments=n)
        ex = jnp.exp(logits - amax[dst])
        denom = jax.ops.segment_sum(ex, dst, num_segments=n)
        alpha = ex / (denom[dst] + 1e-16)
        msg = xl[src] * alpha[..., None]
        out = jax.ops.segment_sum(msg, dst, num_segments=n).reshape(n, HEADS * C) + bias
        mean = out.mean(axis=0)
        var = out.var(axis=0)
        out = (out - mean) * jax.lax.rsqrt(var + BN_EPS) * gamma + beta
        return jax.nn.gelu(out + x, approximate=False)

    def _L1_gnn_ref(x, edge_index, W, b):
        import jax, jax.numpy as jnp
        import numpy as np
        N_NODES = 50000
        N_EDGES = 12500
        D = 64
        N = x.shape[0]
        loops = jnp.arange(N, dtype=edge_index.dtype)
        row = jnp.concatenate([edge_index[0], loops])
        col = jnp.concatenate([edge_index[1], loops])
        ones = jnp.ones(col.shape[0], dtype=x.dtype)
        deg = jax.ops.segment_sum(ones, col, num_segments=N)
        dis = jnp.where(deg > 0, jax.lax.rsqrt(deg), 0.0)
        norm = dis[row] * dis[col]
        h = x @ W
        msgs = h[row] * norm[:, None]
        out = jax.ops.segment_sum(msgs, col, num_segments=N)
        return out + b
    edge_index = jnp.stack([src, dst])
    h = jnp.maximum(_layernorm(x, axis=-1), 0.0)
    x = x + _L0_gnn_ref(h, edge_index, edge_attr_16, L0_gnn_W_l, L0_gnn_b_l, L0_gnn_W_r, L0_gnn_b_r, L0_gnn_W_e, L0_gnn_att, L0_gnn_bias, L0_gnn_gamma, L0_gnn_beta)
    h = jnp.maximum(_layernorm(x, axis=-1), 0.0)
    x = x + _L1_gnn_ref(h, edge_index, L1_gnn_W, L1_gnn_b)
    return x

_drawn_inputs = setup_inputs


def setup_inputs(seed=0):
    import zlib

    import numpy as np

    out = dict(_drawn_inputs(seed))
    spreads = {'L0_gnn_b_l': (0.0, 0.1),
     'L0_gnn_b_r': (0.0, 2.0),
     'L0_gnn_bias': (0.0, 2.0),
     'L0_gnn_gamma': (1.0, 0.2),
     'L0_gnn_beta': (0.0, 0.1),
     'L1_gnn_b': (0.0, 0.1)}
    factors = {'L0_gnn_W_r': 2.674}
    for name, (base, spread) in spreads.items():
        noise = np.random.default_rng([zlib.crc32(name.encode()), seed]).standard_normal(out[name].shape)
        drawn = base * np.exp(spread * noise) if base else spread * noise
        out[name] = jnp.asarray(drawn.astype(out[name].dtype))
    for name, factor in factors.items():
        out[name] = (out[name] * factor).astype(out[name].dtype)
    return out
```

```python
from contextlib import ExitStack

import concourse.bass as bass
from concourse import mybir

F32 = mybir.dt.float32
I32 = mybir.dt.int32
U32 = mybir.dt.uint32
ALU = mybir.AluOpType
ACT = mybir.ActivationFunctionType
AX_X = mybir.AxisListType.X

P = 128
N = 100000
E = 50000
D = 64
ED = 16
H = 4
C = D // H
TILES = 49
BLOCKS = -(-E // (P * TILES))
EP = BLOCKS * P * TILES
GROUP = 7
GROUPS = TILES // GROUP
ALLT = BLOCKS * TILES
CNT = D
DEN = D + 1
REC = D + 1 + H
ROW = D + 1
ROWS = 16
CHUNK = P * ROWS
CHUNKS = -(-N // CHUNK)
LAST0 = N - CHUNK
NT = P * ROWS * CHUNKS
BIG = 1.0e30
SKIP = float(1 << 20)
LN_EPS = 1e-5
BN_EPS = 1e-5
SLOPE = 0.2
RSQRT_MAGIC = float(0x5F3759DF)


def build(nc, x, src, dst, ea, W_l, b_l, W_r, b_r, W_e, att, bias, gamma, beta, W2, b2, agg, x1t, out):
    ctx = ExitStack()
    with ctx:
        def sb(name, shape, dt=F32):
            return ctx.enter_context(nc.sbuf_tensor(name, shape, dt))

        def psum(name, shape):
            return ctx.enter_context(nc.psum_tensor(name, shape, F32))

        def sem(name):
            return ctx.enter_context(nc.semaphore(name))

        waits_passed = sem("waits_passed")

        def wait_alone(eng, signal, count):
            eng.wait_ge(signal, count)
            eng.sem_inc(waits_passed, 1)

        rec_flat = sb("rec", [P, ALLT * REC])
        rec = rec_flat[:, :].rearrange("p (t c) -> p t c", c=REC)
        dst_i = sb("dst_i", [P, ALLT], I32)
        src_i = sb("src_i", [P, ALLT + 2 * GROUP], I32)
        prev_i = sb("prev_i", [P, ALLT], I32)
        next_i = sb("next_i", [P, ALLT], I32)
        row_i = sb("row_i", [P, ALLT], I32)
        dstg_i = sb("dstg_i", [P, ALLT + 2 * GROUP], I32)
        same = sb("same", [P, ALLT])
        first = sb("first", [P, ALLT])
        same_pen = sb("same_pen", [P, ALLT])
        first_pen = sb("first_pen", [P, ALLT])
        is_end = sb("is_end", [P, ALLT])
        dis_dst = sb("dis_dst", [P, ALLT])
        idx_stage = [sb(f"idx_stage{s}", [P, 2 * GROUP], I32) for s in range(2)]
        ident = sb("ident", [P, P])
        ones = sb("ones", [1, P])
        eps = sb("eps", [P, 1])
        w_h = sb("w_h", [P, 2 * D])
        w_ea = sb("w_ea", [GROUP * ED + 2, GROUP * 2 * D])
        w_2 = sb("w_2", [P, 2 * D])
        att_b = sb("att_b", [P, D])
        b2_b = sb("b2_b", [P, D])
        vecs = sb("vecs", [1, 3, D])
        bn = sb("bn", [1, 8, D])
        bn_ab = sb("bn_ab", [1, 2, D])
        bn_b = sb("bn_b", [P, 2, D])
        stat_sum = sb("stat_sum", [1, 2 * D])
        zero = sb("zero", [P, ROWS * ROW])
        ea_in = [sb(f"ea_in{s}", [P, GROUP * ED + 2]) for s in range(2)]
        ea_t = sb("ea_t", [GROUP * ED + 2, P])
        small = sb("small", [P, 4, 2 * GROUP])
        pk = sb("pk", [P, 2, REC])
        pm = sb("pm", [P, 2, H])
        row_m = sb("row_m", [H, 2 * P])
        run_m = sb("run_m", [H, P + 1])
        row_v = sb("row_v", [REC, 2 * P])
        run_v = sb("run_v", [REC, P + 1])
        carry = sb("carry", [P, REC])
        nw = [sb(f"nw{s}", [P, 6, 2 * ROWS]) for s in range(2)]
        work = sb("work", [P, 6 * ROWS * ROW + 5 * ROWS * D])

        def pieces(sizes):
            at, views = 0, []
            for n in sizes:
                views.append(work[:, at:at + n])
                at += n
            return views

        dense = pieces([ROWS * ROW] * 6 + [ROWS * D] * 5)
        xd, ad, od = dense[0:2], dense[2:4], dense[4:6]
        xcd = [v.rearrange("p (r c) -> p r c", c=D) for v in dense[6:8]]
        sqd = dense[8].rearrange("p (r c) -> p r c", c=D)
        hd, gl_flat = dense[9], dense[10]
        gl = gl_flat.rearrange("p (r c) -> p r c", c=D)
        edge = pieces([2 * GROUP * D] * 5 + [GROUP * P, GROUP * D, TILES * D] + [TILES * H] * 5 + [3 * TILES * H, H * (TILES + 1), TILES])
        xg = edge[0:2]
        x1g = [xg[s][:, 0:GROUP * ROW].rearrange("p (t c) -> p t c", c=ROW) for s in range(2)]
        xc, sq = (v.rearrange("p (t c) -> p t c", c=D) for v in edge[2:4])
        hn, hT = edge[4], edge[5]
        zs = edge[6].rearrange("p (t c) -> p t c", c=D)
        wide = edge[7]
        logit, rfac, ffac = (v.rearrange("p (h t) -> p h t", h=H) for v in edge[8:11])
        ffac_t, wide_d = (v.rearrange("p (t h) -> p t h", h=H) for v in edge[11:13])
        expo = edge[13].rearrange("p (j h t) -> p j h t", j=3, h=H)
        mx = edge[14].rearrange("p (h t) -> p h t", h=H)
        end_blk = edge[15]

        ps_t = psum("ps_t", [P, 1024])
        ps_z = psum("ps_z", [P, 1024])
        ps_e = psum("ps_e", [P, 512])
        ps_c = psum("ps_c", [P, 512])
        ps_s = psum("ps_s", [P, 1024])

        def t3(ap, c):
            return ap.rearrange("p (t c) -> p t c", c=c)

        def over_c(ap, n):
            return ap.unsqueeze(len(ap.shape)).to_broadcast(list(ap.shape) + [n])

        def over_r(ap, n):
            return ap.unsqueeze(1).to_broadcast([ap.shape[0], n] + list(ap.shape[1:]))

        edges_in = sem("edges_in")
        weights_in = sem("weights_in")
        cleared = sem("cleared")
        ident_zero = sem("ident_zero")
        setup_done = sem("setup_done")
        agg_zeroed = sem("agg_zeroed")
        with nc.Block() as block:
            @block.sync
            def _(sp):
                def per_edge(ap):
                    return ap.rearrange("(k p t) -> p k t", p=P, t=TILES)

                def tile3(t):
                    return t[:, 0:ALLT].rearrange("p (k t) -> p k t", t=TILES)
                sp.dma_start(tile3(dst_i), per_edge(dst[1:1 + EP])).then_inc(edges_in, 16)
                sp.dma_start(tile3(prev_i), per_edge(dst[0:EP])).then_inc(edges_in, 16)
                sp.dma_start(tile3(next_i), per_edge(dst[2:2 + EP])).then_inc(edges_in, 16)
                sp.dma_start(tile3(src_i), per_edge(src)).then_inc(edges_in, 16)
                sp.wait_ge(cleared, 1)
                for j in range(CHUNKS):
                    sp.dma_start(agg[j * CHUNK:(j + 1) * CHUNK, :].rearrange("(p r) c -> p (r c)", p=P), zero[:, :])\
                        .then_inc(agg_zeroed, 16)

            @block.scalar
            def _(act):
                act.wait_ge(cleared, 4)
                act.dma_start(w_h[0:D, 0:D], W_l).then_inc(weights_in, 16)
                act.dma_start(w_h[0:D, D:2 * D], W_l).then_inc(weights_in, 16)
                act.dma_start(w_h[D:2 * D, D:2 * D], W_r).then_inc(weights_in, 16)
                for j in range(GROUP):
                    act.dma_start(w_ea[j * ED:(j + 1) * ED, j * 2 * D + D:(j + 1) * 2 * D], W_e).then_inc(weights_in, 16)
                k0 = GROUP * ED
                for j in range(GROUP):
                    act.dma_start(w_ea[k0:k0 + 1, j * 2 * D:j * 2 * D + D], b_l.unsqueeze(0)).then_inc(weights_in, 16)
                    act.dma_start(w_ea[k0:k0 + 1, j * 2 * D + D:(j + 1) * 2 * D], b_l.unsqueeze(0)).then_inc(weights_in, 16)
                    act.dma_start(w_ea[k0 + 1:k0 + 2, j * 2 * D + D:(j + 1) * 2 * D], b_r.unsqueeze(0)).then_inc(weights_in, 16)
                act.dma_start(w_2[0:D, 0:D], W2).then_inc(weights_in, 16)
                act.dma_start(w_2[D:2 * D, D:2 * D], W2).then_inc(weights_in, 16)
                act.dma_start(att_b[:, :], att.rearrange("h c -> (h c)").partition_broadcast(P)).then_inc(weights_in, 16)
                act.dma_start(b2_b[:, :], b2.partition_broadcast(P)).then_inc(weights_in, 16)
                for j, v in enumerate((bias, gamma, beta)):
                    act.dma_start(vecs[:, j, :], v.unsqueeze(0)).then_inc(weights_in, 16)
                act.wait_ge(weights_in, 16 * (3 + GROUP + 3 * GROUP + 7))

            @block.gpsimd
            def _(pool):
                pool.memset(ident[:, :], 0.0).then_inc(ident_zero, 1)
                pool.wait_ge(ident_zero, 1)
                pool.affine_select(out=ident[:, :], in_=ident[:, :], compare_op=ALU.not_equal, fill=1.0,
                                   base=0, pattern=[[-1, P]], channel_multiplier=1).then_inc(ident_zero, 1)
                pool.wait_ge(ident_zero, 2)

            @block.vector
            def _(dve):
                dve.memset(zero[:, :], 0.0).then_inc(cleared, 1)
                dve.memset(w_h[:, :], 0.0).then_inc(cleared, 1)
                dve.memset(w_ea[:, :], 0.0).then_inc(cleared, 1)
                dve.memset(w_2[:, :], 0.0).then_inc(cleared, 1)
                dve.memset(ones[:, :], 1.0)
                dve.memset(eps[:, :], LN_EPS)
                dve.memset(stat_sum[:, :], 0.0)
                dve.memset(run_m[:, :], -BIG)
                dve.memset(run_v[:, :], 0.0)
                for s in range(2):
                    dve.memset(ea_in[s][:, GROUP * ED:GROUP * ED + 2], 1.0)
                dve.memset(src_i[:, ALLT:ALLT + 2 * GROUP], 0)
                dve.memset(dstg_i[:, ALLT:ALLT + 2 * GROUP], 0)
                dve.wait_ge(edges_in, 64)
                dve.tensor_tensor(same[:, :], dst_i[:, :], prev_i[:, :], ALU.is_equal)
                dve.tensor_tensor(is_end[:, :], dst_i[:, :], next_i[:, :], ALU.not_equal)
                before = t3(prev_i[:, :], TILES)[:, :, 0]
                dve.tensor_tensor(t3(first[:, :], TILES), t3(dst_i[:, :], TILES), over_c(before, TILES), ALU.is_equal)
                dve.tensor_scalar(dstg_i[:, 0:ALLT], dst_i[:, :], float(N - 1), None, ALU.min)
                dve.drain()
                dve.tensor_scalar(same_pen[:, :], same[:, :], -1.0, BIG, ALU.add, ALU.mult)
                dve.tensor_scalar(first_pen[:, :], first[:, :], -1.0, BIG, ALU.add, ALU.mult)
                dve.tensor_scalar(dis_dst[:, :], is_end[:, :], -SKIP, SKIP, ALU.mult, ALU.add)
                dve.drain()
                dve.tensor_tensor(row_i[:, :], dst_i[:, :], dis_dst[:, :], ALU.add)
                dve.drain()

        def slot_use(k, g):
            return k * (GROUPS - GROUPS // 2) + g // 2 if g % 2 == 0 else k * (GROUPS // 2) + g // 2

        def scan_over_partitions(dve, row, run, n, op0, op1, ps):
            dve.tensor_copy(row[0:n, :], ps[0:n, 0:2 * P])
            dve.tensor_copy(run[0:n, 0:1], run[0:n, P:P + 1])
            dve.drain()
            return dve.tensor_tensor_scan(run[0:n, 1:P + 1], row[0:n, P:2 * P], row[0:n, 0:P], run[0:n, 0:1], op0, op1)

        idx_staged = sem("idx_staged")
        gathered = [sem(f"gathered{s}") for s in range(2)]
        xg_free = [sem(f"xg_free{s}") for s in range(2)]
        ea_landed = [sem(f"ea_landed{s}") for s in range(2)]
        ea_turned = [sem(f"ea_turned{s}") for s in range(2)]
        centered = sem("centered")
        squared = sem("squared")
        summed = sem("summed")
        std_ready = sem("std_ready")
        h_ready = sem("h_ready")
        hT_psum = sem("hT_psum")
        hT_ready = sem("hT_ready")
        ea_t_ready = sem("ea_t_ready")
        z_psum = sem("z_psum")
        z_ready = sem("z_ready")
        zs_free = sem("zs_free")
        max_rows = sem("max_rows")
        max_rows_t = sem("max_rows_t")
        max_run = sem("max_run")
        max_carry = sem("max_carry")
        expo_in = sem("expo_in")
        expo_out = sem("expo_out")
        sum_rows = sem("sum_rows")
        sum_rows_t = sem("sum_rows_t")
        sum_run = sem("sum_run")
        sum_carry = sem("sum_carry")
        o_ready = sem("o_ready")
        o_squared = sem("o_squared")
        stats_psum = sem("stats_psum")
        with nc.Block() as block:
            @block.sync
            def _(sp):
                ea_r = ea.rearrange("(k p t) c -> k p (t c)", p=P, t=TILES)
                with sp.Fori(0, BLOCKS) as k:
                    for g in range(GROUPS):
                        s, use = g % 2, slot_use(k, g)
                        sp.wait_ge(ea_turned[s], use + 1)
                        sp.dma_start(ea_in[s][:, 0:GROUP * ED],
                                     ea_r[bass.ds(k, 1), :, g * GROUP * ED:(g + 1) * GROUP * ED]
                                     .rearrange("k p c -> p (k c)")).then_inc(ea_landed[s], 16)

            @block.gpsimd
            def _(pool):
                with pool.Fori(0, BLOCKS) as k:
                    for g in range(GROUPS):
                        s, use = g % 2, slot_use(k, g)
                        wait_alone(pool, idx_staged, k * GROUPS + (g + 1))
                        wait_alone(pool, xg_free[s], use + 1)
                        for t in range(GROUP):
                            for side in range(2):
                                a = (2 * t + side) * D
                                i = side * GROUP + t
                                pool.indirect_dma_start(
                                    xg[s][:, a:a + D], None, x,
                                    bass.IndirectOffsetOnAxis(ap=idx_stage[s][:, i:i + 1].bitcast(U32), axis=0),
                                    bounds_check=N - 1, oob_is_err=False).then_inc(gathered[s], 16)

            @block.scalar
            def _(act):
                with act.Fori(0, BLOCKS) as k:
                    for g in range(GROUPS):
                        s, use, n = g % 2, slot_use(k, g), k * GROUPS + (g + 1)
                        act.wait_ge(centered, n)
                        act.activation(sq[:, :, :], xc[:, :, :], ACT.Square).then_inc(squared, 1)
                        act.wait_ge(summed, n)
                        act.activation(small[:, 2, :], small[:, 1, :], ACT.Sqrt, bias=eps[:, :],
                                       scale=1.0 / D).then_inc(std_ready, 1)
                        act.wait_ge(ea_turned[s], use + 2)
                        act.activation(ea_t[:, :], ps_e[0:GROUP * ED + 2, 0:P], ACT.Copy).then_inc(ea_t_ready, 1)
                        act.wait_ge(hT_psum, n)
                        act.activation(hT[:, :], ps_t[:, 0:GROUP * P], ACT.Copy).then_inc(hT_ready, 1)
                        wait_alone(act, z_psum, n)
                        z = t3(ps_z[:, 0:GROUP * 2 * D], 2 * D)
                        act.activation(rec[:, bass.ds(k * TILES + g * GROUP, GROUP), 0:D], z[:, :, 0:D], ACT.Copy)
                        act.wait_ge(zs_free, n)
                        act.activation(zs[:, :, :], z[:, :, D:2 * D], ACT.Copy).then_inc(z_ready, 1)
                    act.wait_ge(expo_in, k + 1)
                    act.activation(expo[:, :, :, :], expo[:, :, :, :], ACT.Exp).then_inc(expo_out, 1)
                    wait_alone(act, o_ready, k + 1)
                    act.activation(t3(wide[:, :], D), rec[:, bass.ds(k * TILES, TILES), 0:D], ACT.Square).then_inc(o_squared, 1)

            @block.tensor
            def _(pe):
                for s in range(2):
                    pe.sem_inc(ea_turned[s], 1)
                with pe.Fori(0, BLOCKS) as k:
                    for g in range(GROUPS):
                        s, use, n = g % 2, slot_use(k, g), k * GROUPS + (g + 1)
                        pe.wait_ge(ea_landed[s], (use + 1) * 16)
                        pe.transpose(ps_e[0:GROUP * ED + 2, 0:P], ea_in[s][:, :], ident[:, :]).then_inc(ea_turned[s], 1)
                        pe.wait_ge(h_ready, n)
                        for t in range(GROUP):
                            last = pe.transpose(ps_t[:, t * P:(t + 1) * P], hn[:, t * P:(t + 1) * P], ident[:, :])
                        last.then_inc(hT_psum, 1)
                        pe.wait_ge(ea_t_ready, n)
                        for a, b in ((0, 4), (4, GROUP)):
                            pe.matmul(ps_z[:, a * P:b * P], ea_t[:, :], w_ea[:, a * P:b * P], start=True, stop=False,
                                      skip_group_check=True)
                        pe.wait_ge(hT_ready, n)
                        for t in range(GROUP):
                            last = pe.matmul(ps_z[:, t * P:(t + 1) * P], hT[:, t * P:(t + 1) * P], w_h[:, :],
                                             start=False, stop=True, skip_group_check=True)
                        last.then_inc(z_psum, 1)
                    wait_alone(pe, max_rows, k + 1)
                    for j in range(2):
                        last = pe.transpose(ps_c[0:H, j * P:(j + 1) * P], pm[:, j, :], ident[:, :])
                    last.then_inc(max_rows_t, 1)
                    wait_alone(pe, max_run, k + 1)
                    pe.transpose(ps_e[:, 0:H], run_m[:, 0:P], ident[0:H, 0:H]).then_inc(max_carry, 1)
                    wait_alone(pe, sum_rows, k + 1)
                    for j in range(2):
                        last = pe.transpose(ps_c[0:REC, j * P:(j + 1) * P], pk[:, j, :], ident[:, :])
                    last.then_inc(sum_rows_t, 1)
                    wait_alone(pe, sum_run, k + 1)
                    pe.transpose(ps_e[:, 0:REC], run_v[:, 0:P], ident[0:REC, 0:REC]).then_inc(sum_carry, 1)
                    pe.wait_ge(o_squared, k + 1)
                    for j, base in ((0, None), (1, wide)):
                        for t in range(TILES):
                            rhs = rec[:, bass.ds(k * TILES + t, 1), 0:D].rearrange("p t c -> p (t c)") if j == 0 else \
                                wide[:, t * D:(t + 1) * D]
                            last = pe.matmul(ps_s[0:1, j * 512:j * 512 + D], end_blk[:, t:t + 1], rhs,
                                             start=(t == 0), stop=(t == TILES - 1))
                    last.then_inc(stats_psum, 1)

            @block.vector
            def _(dve):
                def stage_indices(k, g, s):
                    a = k * TILES + g * GROUP
                    dve.tensor_copy(idx_stage[s][:, 0:GROUP], src_i[:, bass.ds(a, GROUP)])
                    dve.tensor_copy(idx_stage[s][:, GROUP:2 * GROUP], dstg_i[:, bass.ds(a, GROUP)]).then_inc(idx_staged, 1)

                def layer_norm(k, g):
                    s, use, n = g % 2, slot_use(k, g), k * GROUPS + (g + 1)
                    dve.wait_ge(gathered[s], (use + 1) * (2 * GROUP * 16))
                    if g + 2 < GROUPS:
                        stage_indices(k, g + 2, s)
                    rows = t3(xg[s][:, :], D)
                    dve.reduce_sum(small[:, 0, :], rows, AX_X)
                    dve.drain()
                    dve.tensor_scalar(small[:, 0, :], small[:, 0, :], -1.0 / D, None, ALU.mult)
                    dve.drain()
                    dve.tensor_tensor(xc[:, :, :], rows, over_c(small[:, 0, :], D), ALU.add).then_inc(centered, 1)
                    dve.drain().then_inc(xg_free[s], 1)

                def normalize(k, g):
                    n = k * GROUPS + (g + 1)
                    dve.wait_ge(squared, n)
                    dve.reduce_sum(small[:, 1, :], sq[:, :, :], AX_X).then_inc(summed, 1)
                    dve.wait_ge(std_ready, n)
                    dve.reciprocal(small[:, 3, :], small[:, 2, :])
                    dve.drain()
                    dve.scalar_tensor_tensor(out=t3(hn[:, :], D), in0=xc[:, :, :], scalar=0.0,
                                             in1=over_c(small[:, 3, :], D), op0=ALU.max, op1=ALU.mult).then_inc(h_ready, 1)

                def logits(k, g):
                    n = k * GROUPS + (g + 1)
                    dve.wait_ge(z_ready, n)
                    dve.scalar_tensor_tensor(out=sq[:, 0:GROUP, :], in0=zs[:, :, :], scalar=SLOPE, in1=zs[:, :, :],
                                             op0=ALU.mult, op1=ALU.max)
                    dve.drain().then_inc(zs_free, 1)
                    dve.tensor_tensor(sq[:, GROUP:2 * GROUP, :], sq[:, 0:GROUP, :], over_r(att_b[:, :], GROUP), ALU.mult)
                    dve.drain()
                    dve.reduce_sum(logit[:, :, g * GROUP:(g + 1) * GROUP].rearrange("p h t -> p t h"),
                                   sq[:, GROUP:2 * GROUP, :].rearrange("p t (h c) -> p t h c", h=H), AX_X)
                    dve.drain()

                for s in range(2):
                    dve.sem_inc(xg_free[s], 1)
                    stage_indices(0, s, s)
                dve.sem_inc(zs_free, 1)
                with dve.Fori(0, BLOCKS) as k:
                    blk = bass.ds(k * TILES, TILES)
                    for g in range(GROUPS):
                        layer_norm(k, g)
                        normalize(k, g)
                        logits(k, g)
                    a = (k + 1) * TILES
                    for s in range(2):
                        dve.tensor_copy(idx_stage[s][:, 0:GROUP], src_i[:, bass.ds(a + s * GROUP, GROUP)])
                        dve.tensor_copy(idx_stage[s][:, GROUP:2 * GROUP],
                                        dstg_i[:, bass.ds(a + s * GROUP, GROUP)]).then_inc(idx_staged, 1)
                    for h in range(H):
                        dve.tensor_tensor_scan(mx[:, h, 1:TILES + 1], same_pen[:, blk], logit[:, h, :], -BIG,
                                               ALU.add, ALU.max)
                    dve.drain()
                    dve.tensor_copy(pm[:, 0, :], mx[:, :, TILES])
                    dve.tensor_copy(pm[:, 1, :], first_pen[:, bass.ds(k * TILES + TILES - 1, 1)].to_broadcast([P, H]))\
                        .then_inc(max_rows, 1)
                    dve.wait_ge(max_rows_t, k + 1)
                    scan_over_partitions(dve, row_m, run_m, H, ALU.add, ALU.max, ps_c).then_inc(max_run, 1)
                    dve.wait_ge(max_carry, k + 1)
                    dve.tensor_copy(mx[:, :, 0], ps_e[:, 0:H])
                    dve.drain()
                    came = over_c(mx[:, :, 0], TILES)
                    dve.tensor_tensor(rfac[:, :, :], came, over_r(first_pen[:, blk], H), ALU.add)
                    dve.drain()
                    dve.tensor_tensor(mx[:, :, 1:TILES + 1], mx[:, :, 1:TILES + 1], rfac[:, :, :], ALU.max)
                    dve.drain()
                    now = mx[:, :, 1:TILES + 1]
                    dve.tensor_tensor(expo[:, 0, :, :], mx[:, :, 0:TILES], now, ALU.subtract)
                    dve.tensor_tensor(expo[:, 1, :, :], came, now, ALU.subtract)
                    dve.tensor_tensor(expo[:, 2, :, :], logit[:, :, :], now, ALU.subtract)
                    dve.drain()
                    dve.tensor_scalar(expo[:, :, :, :], expo[:, :, :, :], 0.0, None, ALU.min).then_inc(expo_in, 1)
                    dve.wait_ge(expo_out, k + 1)
                    dve.tensor_tensor(rfac[:, :, :], expo[:, 0, :, :], over_r(same[:, blk], H), ALU.mult)
                    dve.tensor_tensor(ffac[:, :, :], expo[:, 1, :, :], over_r(first[:, blk], H), ALU.mult)
                    ex_t = expo[:, 2, :, :].rearrange("p h t -> p t h")
                    heads = rec[:, blk, 0:D].rearrange("p t (h c) -> p t h c", h=H)
                    dve.tensor_tensor(heads, heads, over_c(ex_t, C), ALU.mult)
                    dve.tensor_copy(rec[:, blk, DEN:DEN + H], ex_t)
                    dve.tensor_scalar(rec[:, blk, CNT], same[:, blk], 0.0, 1.0, ALU.mult, ALU.add)
                    dve.tensor_copy(end_blk[:, :], is_end[:, blk])
                    dve.drain()
                    for c in range(REC):
                        decay = same[:, blk] if c == CNT else rfac[:, c // C if c < D else c - DEN, :]
                        col = rec[:, blk, c]
                        dve.tensor_tensor_scan(col, decay, col, 0.0, ALU.mult, ALU.add)
                    dve.drain()
                    at_end = bass.ds(k * TILES + TILES - 1, 1)
                    dve.tensor_copy(pk[:, 0, :], rec[:, at_end, :].rearrange("p t c -> p (t c)"))
                    last = ffac[:, :, TILES - 1]
                    dve.tensor_copy(pk[:, 1, 0:D].rearrange("p (h c) -> p h c", h=H), over_c(last, C))
                    dve.tensor_copy(pk[:, 1, DEN:DEN + H], last)
                    dve.tensor_copy(pk[:, 1, CNT:CNT + 1], first[:, at_end])
                    dve.tensor_copy(ffac_t[:, :, :], ffac[:, :, :].rearrange("p h t -> p t h"))
                    dve.drain().then_inc(sum_rows, 1)
                    dve.wait_ge(sum_rows_t, k + 1)
                    scan_over_partitions(dve, row_v, run_v, REC, ALU.mult, ALU.add, ps_c).then_inc(sum_run, 1)
                    dve.wait_ge(sum_carry, k + 1)
                    dve.tensor_copy(carry[:, :], ps_e[:, 0:REC])
                    dve.drain()
                    w4 = wide[:, :].rearrange("p (t h c) -> p t h c", h=H, c=C)
                    dve.tensor_tensor(w4, over_c(ffac_t[:, :, :], C),
                                      over_r(carry[:, 0:D].rearrange("p (h c) -> p h c", h=H), TILES), ALU.mult)
                    dve.tensor_tensor(wide_d[:, :, :], ffac_t[:, :, :], over_r(carry[:, DEN:DEN + H], TILES), ALU.mult)
                    dve.scalar_tensor_tensor(out=rec[:, blk, CNT], in0=first[:, blk], scalar=carry[:, CNT:CNT + 1],
                                             in1=rec[:, blk, CNT], op0=ALU.mult, op1=ALU.add)
                    dve.drain()
                    dve.tensor_tensor(rec[:, blk, 0:D], rec[:, blk, 0:D], t3(wide[:, :], D), ALU.add)
                    dve.scalar_tensor_tensor(out=wide_d[:, :, :], in0=wide_d[:, :, :], scalar=1e-16,
                                             in1=rec[:, blk, DEN:DEN + H], op0=ALU.add, op1=ALU.add)
                    dve.drain()
                    dve.reciprocal(wide_d[:, :, :], wide_d[:, :, :])
                    dve.drain()
                    dve.tensor_tensor(heads, heads, over_c(wide_d[:, :, :], C), ALU.mult).then_inc(o_ready, 1)
                    dve.wait_ge(stats_psum, k + 1)
                    both = ps_s[0:1, :].rearrange("p (j c) -> p j c", c=512)[:, :, 0:D]
                    ss = t3(stat_sum[:, :], D)
                    dve.tensor_tensor(ss, ss, both, ALU.add)
                    dve.drain()

        cnt_std = sem("cnt_std")
        bn_var = sem("bn_var")
        bn_std = sem("bn_std")
        bn_row = sem("bn_row")
        bn_psum = sem("bn_psum")
        o_stored = sem("o_stored")
        with nc.Block() as block:
            @block.gpsimd
            def _(pool):
                pool.wait_ge(agg_zeroed, 16 * CHUNKS)
                for t in range(ALLT):
                    pool.indirect_dma_start(
                        agg, bass.IndirectOffsetOnAxis(ap=row_i[:, t:t + 1].bitcast(U32), axis=0),
                        rec[:, t, 0:ROW], None, bounds_check=N - 1, oob_is_err=False).then_inc(o_stored, 16)
                pool.wait_ge(o_stored, 16 * ALLT)

            @block.vector
            def _(dve):
                mean, var, sq_m, rstd = (bn[:, j, :] for j in range(4))
                dve.tensor_scalar(mean, stat_sum[:, 0:D], 1.0 / N, None, ALU.mult)
                dve.drain()
                dve.tensor_tensor(sq_m, mean, mean, ALU.mult)
                dve.drain()
                dve.scalar_tensor_tensor(out=var, in0=stat_sum[:, D:2 * D], scalar=1.0 / N, in1=sq_m,
                                         op0=ALU.mult, op1=ALU.subtract).then_inc(bn_var, 1)
                dve.wait_ge(bn_std, 1)
                dve.reciprocal(rstd, bn[:, 4, :])
                dve.drain()
                dve.tensor_tensor(bn_ab[:, 0, :], rstd, vecs[:, 1, :], ALU.mult)
                dve.tensor_tensor(bn[:, 5, :], mean, vecs[:, 0, :], ALU.add)
                dve.drain()
                dve.tensor_tensor(bn[:, 6, :], vecs[:, 0, :], bn[:, 5, :], ALU.subtract)
                dve.drain()
                dve.tensor_tensor(bn[:, 7, :], bn[:, 6, :], bn_ab[:, 0, :], ALU.mult)
                dve.drain()
                dve.tensor_tensor(bn_ab[:, 1, :], bn[:, 7, :], vecs[:, 2, :], ALU.add).then_inc(bn_row, 1)
                dve.wait_ge(bn_psum, 1)
                dve.tensor_copy(bn_b[:, :, :], ps_c[:, 0:2 * D].rearrange("p (j c) -> p j c", c=D))
                dve.wait_ge(cnt_std, 1)
                dve.reciprocal(dis_dst[:, :], dis_dst[:, :])
                dve.drain()

            @block.scalar
            def _(act):
                act.wait_ge(bn_var, 1)
                act.activation(bn[:, 4, :], bn[:, 1, :], ACT.Sqrt, bias=eps[0:1, :], scale=1.0).then_inc(bn_std, 1)
                act.activation(dis_dst[:, :], rec[:, :, CNT], ACT.Copy, bias=1.0, scale=1.0)
                act.drain()
                act.activation(dis_dst[:, :], dis_dst[:, :], ACT.Sqrt).then_inc(cnt_std, 1)

            @block.tensor
            def _(pe):
                pe.wait_ge(bn_row, 1)
                pe.matmul(ps_c[:, 0:2 * D], ones[:, :], bn_ab[:, :, :].rearrange("p j c -> p (j c)"),
                          start=True, stop=True).then_inc(bn_psum, 1)

        def chunk_at(ap, w, n):
            start = LAST0 if isinstance(n, int) and n == CHUNKS - 1 else n * CHUNK
            return ap[bass.ds(start, CHUNK), :].rearrange("(p r) c -> p (r c)", p=P)

        def over_chunks(eng, step):
            with eng.Fori(0, (CHUNKS - 1) // 2) as i:
                step(i * 2 + 1, 1, i)
                step(i * 2 + 2, 0, i + 1)

        def dense_sems(tag):
            return dict(landed=[sem(f"{tag}_landed{s}") for s in range(2)], free=[sem(f"{tag}_free{s}") for s in range(2)],
                        made=[sem(f"{tag}_made{s}") for s in range(2)], stored=[sem(f"{tag}_stored{s}") for s in range(2)],
                        centered=sem(f"{tag}_centered"), squared=sem(f"{tag}_squared"), var=sem(f"{tag}_var"),
                        rstd=sem(f"{tag}_rstd"), z=sem(f"{tag}_z"), act=sem(f"{tag}_act"), gl_free=sem(f"{tag}_gl_free"))

        def dense_loads(sp, q, a, wa, ta, b, wb, tb):
            def load(n, s, u):
                sp.wait_ge(q["free"][s], u + 1)
                sp.dma_start(ta[s][:, 0:ROWS * wa], chunk_at(a, wa, n)).then_inc(q["landed"][s], 16)
                sp.dma_start(tb[s][:, 0:ROWS * wb], chunk_at(b, wb, n)).then_inc(q["landed"][s], 16)
            with sp.Fori(0, (CHUNKS - 1) // 2) as i:
                load(i * 2, 0, i)
                load(i * 2 + 1, 1, i)
            load(CHUNKS - 1, 0, (CHUNKS - 1) // 2)

        q = dense_sems("x1")
        newton_step = sem("newton_step")
        with nc.Block() as block:
            @block.sync
            def _(sp):
                dense_loads(sp, q, x, D, xd, agg, ROW, ad)

            @block.gpsimd
            def _(pool):
                def newton(n, s, u):
                    v, y, a, b = (nw[s][:, j, :] for j in range(4))
                    wait_alone(pool, q["var"], n + 1)
                    for _ in range(3):
                        pool.tensor_tensor(a, y, y, ALU.mult)
                        pool.drain()
                        pool.tensor_tensor(b, a, v, ALU.mult)
                        pool.drain()
                        pool.tensor_scalar(a, b, -0.5, 1.5, ALU.mult, ALU.add)
                        pool.drain()
                        pool.tensor_tensor(y, y, a, ALU.mult)
                        pool.drain()
                    pool.sem_inc(q["rstd"], 1)

                def finish(n, s, u):
                    wait_alone(pool, q["act"], n + 2)
                    if not (isinstance(u, int) and u == 0):
                        wait_alone(pool, q["stored"][s], u * 16)
                    rows = t3(od[s][:, :], ROW)
                    pool.tensor_copy(rows[:, :, D:D + 1], nw[s][:, 1, ROWS:2 * ROWS].unsqueeze(2))
                    pool.tensor_tensor(rows[:, :, 0:D], t3(xd[s][:, 0:ROWS * D], D), gl[:, :, :], ALU.add)
                    pool.drain().then_inc(q["made"][s], 1)
                    pool.drain().then_inc(q["free"][s], 1)
                    pool.drain().then_inc(q["gl_free"], 1)

                for s in range(2):
                    pool.sem_inc(q["free"][s], 1)
                pool.sem_inc(q["gl_free"], 1)
                half = (CHUNKS - 1) // 2
                newton(0, 0, 0)
                newton(1, 1, 0)
                finish(0, 0, 0)
                newton(2, 0, 1)
                finish(1, 1, 0)
                with pool.Fori(1, half) as i:
                    newton(i * 2 + 1, 1, i)
                    finish(i * 2, 0, i)
                    newton(i * 2 + 2, 0, i + 1)
                    finish(i * 2 + 1, 1, i)
                finish(CHUNKS - 1, 0, half)

            @block.vector
            def _(dve):
                def center(n, s, u):
                    dve.wait_ge(q["landed"][s], (u + 1) * 32)
                    rows = t3(xd[s][:, 0:ROWS * D], D)
                    m = nw[s][:, 4, 0:ROWS]
                    dve.reduce_sum(m, rows, AX_X)
                    dve.drain()
                    dve.tensor_scalar(m, m, -1.0 / D, None, ALU.mult)
                    dve.drain()
                    dve.tensor_tensor(xcd[s], rows, over_c(m, D), ALU.add).then_inc(q["centered"], 1)

                def variance(n, s, u):
                    v, y = nw[s][:, 0, :], nw[s][:, 1, :]
                    dve.wait_ge(q["squared"], n + 1)
                    dve.reduce_sum(nw[s][:, 5, 0:ROWS], sqd[:, :, :], AX_X)
                    dve.tensor_scalar(v[:, ROWS:2 * ROWS], t3(ad[s][:, :], ROW)[:, :, CNT], 1.0, None, ALU.add)
                    dve.drain()
                    dve.tensor_scalar(v[:, 0:ROWS], nw[s][:, 5, 0:ROWS], 1.0 / D, LN_EPS, ALU.mult, ALU.add)
                    dve.drain()
                    half = nw[s][:, 2, :].bitcast(I32)
                    dve.tensor_scalar(half, v.bitcast(I32), 1, None, ALU.arith_shift_right)
                    dve.drain()
                    dve.tensor_scalar(y.bitcast(I32), half, -1.0, RSQRT_MAGIC, ALU.mult, ALU.add).then_inc(q["var"], 1)

                def combine(n, s, u):
                    dve.wait_ge(q["act"], n + 1)
                    dve.wait_ge(q["rstd"], n + 1)
                    h = t3(hd[:, :], D)
                    o = t3(ad[s][:, :], ROW)[:, :, 0:D]
                    dve.scalar_tensor_tensor(out=h, in0=xcd[s], scalar=0.0, in1=over_c(nw[s][:, 1, 0:ROWS], D),
                                             op0=ALU.max, op1=ALU.mult)
                    dve.tensor_tensor(o, o, over_r(bn_b[:, 0, :], ROWS), ALU.mult)
                    dve.drain()
                    dve.tensor_tensor(h, h, o, ALU.add)
                    dve.drain()
                    dve.tensor_tensor(h, h, over_r(bn_b[:, 1, :], ROWS), ALU.add).then_inc(q["z"], 1)

                center(0, 0, 0)
                variance(0, 0, 0)
                with dve.Fori(0, (CHUNKS - 1) // 2) as i:
                    center(i * 2 + 1, 1, i)
                    combine(i * 2, 0, i)
                    variance(i * 2 + 1, 1, i)
                    center(i * 2 + 2, 0, i + 1)
                    combine(i * 2 + 1, 1, i)
                    variance(i * 2 + 2, 0, i + 1)
                combine(CHUNKS - 1, 0, (CHUNKS - 1) // 2)

            @block.scalar
            def _(act):
                def square(n, s, u):
                    act.wait_ge(q["centered"], n + 1)
                    act.activation(sqd[:, :, :], xcd[s], ACT.Square).then_inc(q["squared"], 1)

                def gelu(n, s, u):
                    act.wait_ge(q["gl_free"], n + 1)
                    act.wait_ge(q["z"], n + 1)
                    act.activation(gl[:, :, :], t3(hd[:, :], D), ACT.Gelu).then_inc(q["act"], 1)

                def store(n, s, u):
                    act.wait_ge(q["made"][s], u + 1)
                    act.dma_start(chunk_at(x1t, ROW, n), od[s][:, :]).then_inc(q["stored"][s], 16)

                act.sem_inc(q["act"], 1)
                square(0, 0, 0)
                square(1, 1, 0)
                gelu(0, 0, 0)
                square(2, 0, 1)
                gelu(1, 1, 0)
                store(0, 0, 0)
                with act.Fori(1, (CHUNKS - 1) // 2) as i:
                    square(i * 2 + 1, 1, i)
                    gelu(i * 2, 0, i)
                    store(i * 2 - 1, 1, i - 1)
                    square(i * 2 + 2, 0, i + 1)
                    gelu(i * 2 + 1, 1, i)
                    store(i * 2, 0, i)
                half = (CHUNKS - 1) // 2
                gelu(CHUNKS - 1, 0, half)
                store(CHUNKS - 2, 1, half - 1)
                act.wait_ge(q["stored"][1], 16 * half)
                store(CHUNKS - 1, 0, half)
                act.wait_ge(q["stored"][0], 16 * (half + 1))

        idx2_staged = sem("idx2_staged")
        gathered2 = [sem(f"gathered2_{s}") for s in range(2)]
        x1g_free = [sem(f"x1g_free{s}") for s in range(2)]
        centered2 = sem("centered2")
        squared2 = sem("squared2")
        summed2 = sem("summed2")
        std2_ready = sem("std2_ready")
        rows2 = sem("rows2")
        rows2_t = sem("rows2_t")
        run2 = sem("run2")
        carry2 = sem("carry2")
        with nc.Block() as block:
            @block.gpsimd
            def _(pool):
                with pool.Fori(0, BLOCKS) as k:
                    for g in range(GROUPS):
                        s, use = g % 2, slot_use(k, g)
                        wait_alone(pool, idx2_staged, k * GROUPS + (g + 1))
                        wait_alone(pool, x1g_free[s], use + 1)
                        for t in range(GROUP):
                            pool.indirect_dma_start(
                                xg[s][:, t * ROW:(t + 1) * ROW], None, x1t,
                                bass.IndirectOffsetOnAxis(ap=idx_stage[s][:, t:t + 1].bitcast(U32), axis=0),
                                bounds_check=N - 1, oob_is_err=False).then_inc(gathered2[s], 16)

            @block.scalar
            def _(act):
                with act.Fori(0, BLOCKS) as k:
                    for g in range(GROUPS):
                        n = k * GROUPS + (g + 1)
                        act.wait_ge(centered2, n)
                        act.activation(sq[:, 0:GROUP, :], xc[:, 0:GROUP, :], ACT.Square).then_inc(squared2, 1)
                        act.wait_ge(summed2, n)
                        act.activation(small[:, 2, 0:GROUP], small[:, 1, 0:GROUP], ACT.Sqrt, bias=eps[:, :],
                                       scale=1.0 / D).then_inc(std2_ready, 1)

            @block.tensor
            def _(pe):
                with pe.Fori(0, BLOCKS) as k:
                    wait_alone(pe, rows2, k + 1)
                    for j in range(2):
                        last = pe.transpose(ps_c[0:D, j * P:(j + 1) * P], pk[:, j, 0:D], ident[:, :])
                    last.then_inc(rows2_t, 1)
                    wait_alone(pe, run2, k + 1)
                    pe.transpose(ps_e[:, 0:D], run_v[0:D, 0:P], ident[0:D, 0:D]).then_inc(carry2, 1)

            @block.vector
            def _(dve):
                dve.memset(run_v[:, :], 0.0)
                for s in range(2):
                    dve.sem_inc(x1g_free[s], 1)
                    dve.tensor_copy(idx_stage[s][:, 0:GROUP], src_i[:, s * GROUP:(s + 1) * GROUP]).then_inc(idx2_staged, 1)
                with dve.Fori(0, BLOCKS) as k:
                    blk = bass.ds(k * TILES, TILES)
                    for g in range(GROUPS):
                        s, use, n = g % 2, slot_use(k, g), k * GROUPS + (g + 1)
                        dve.wait_ge(gathered2[s], (use + 1) * (GROUP * 16))
                        if g + 2 < GROUPS:
                            dve.tensor_copy(idx_stage[s][:, 0:GROUP], src_i[:, bass.ds(k * TILES + (g + 2) * GROUP, GROUP)])\
                                .then_inc(idx2_staged, 1)
                        rows = x1g[s][:, :, 0:D]
                        m = small[:, 0, 0:GROUP]
                        dve.reduce_sum(m, rows, AX_X)
                        dve.drain()
                        dve.tensor_scalar(m, m, -1.0 / D, None, ALU.mult)
                        dve.drain()
                        dve.tensor_tensor(xc[:, 0:GROUP, :], rows, over_c(m, D), ALU.add).then_inc(centered2, 1)
                        dve.wait_ge(squared2, n)
                        dve.reduce_sum(small[:, 1, 0:GROUP], sq[:, 0:GROUP, :], AX_X).then_inc(summed2, 1)
                        dve.wait_ge(std2_ready, n)
                        r = small[:, 3, 0:GROUP]
                        dve.reciprocal(r, small[:, 2, 0:GROUP])
                        dve.drain()
                        dve.tensor_tensor(r, r, x1g[s][:, :, D], ALU.mult)
                        dve.drain().then_inc(x1g_free[s], 1)
                        dve.scalar_tensor_tensor(out=rec[:, bass.ds(k * TILES + g * GROUP, GROUP), 0:D],
                                                 in0=xc[:, 0:GROUP, :], scalar=0.0, in1=over_c(r, D),
                                                 op0=ALU.max, op1=ALU.mult)
                    a = (k + 1) * TILES
                    for s in range(2):
                        dve.tensor_copy(idx_stage[s][:, 0:GROUP], src_i[:, bass.ds(a + s * GROUP, GROUP)])\
                            .then_inc(idx2_staged, 1)
                    dve.drain()
                    for c in range(D):
                        col = rec[:, blk, c]
                        dve.tensor_tensor_scan(col, same[:, blk], col, 0.0, ALU.mult, ALU.add)
                    dve.drain()
                    at_end = bass.ds(k * TILES + TILES - 1, 1)
                    dve.tensor_copy(pk[:, 0, 0:D], rec[:, at_end, 0:D].rearrange("p t c -> p (t c)"))
                    dve.tensor_copy(pk[:, 1, 0:D], first[:, at_end].to_broadcast([P, D]))
                    dve.drain().then_inc(rows2, 1)
                    dve.wait_ge(rows2_t, k + 1)
                    scan_over_partitions(dve, row_v, run_v, D, ALU.mult, ALU.add, ps_c).then_inc(run2, 1)
                    dve.wait_ge(carry2, k + 1)
                    dve.tensor_copy(carry[:, 0:D], ps_e[:, 0:D])
                    dve.drain()
                    w3 = t3(wide[:, :], D)
                    dve.tensor_tensor(w3, over_c(first[:, blk], D), over_r(carry[:, 0:D], TILES), ALU.mult)
                    dve.drain()
                    dve.tensor_tensor(w3, w3, rec[:, blk, 0:D], ALU.add)
                    dve.drain()
                    dve.tensor_tensor(rec[:, blk, 0:D], w3, over_c(dis_dst[:, blk], D), ALU.mult)
                    dve.drain()

        m_stored = sem("m_stored")
        with nc.Block() as block:
            @block.gpsimd
            def _(pool):
                for t in range(ALLT):
                    pool.indirect_dma_start(
                        agg, bass.IndirectOffsetOnAxis(ap=row_i[:, t:t + 1].bitcast(U32), axis=0),
                        rec[:, t, 0:ROW], None, bounds_check=N - 1, oob_is_err=False).then_inc(m_stored, 16)
                pool.wait_ge(m_stored, 16 * ALLT)

        r_ = dense_sems("out")
        s_psum = sem("s_psum")
        sT_ready = sem("sT_ready")
        y_psum = sem("y_psum")
        xb_ready = sem("xb_ready")
        with nc.Block() as block:
            @block.sync
            def _(sp):
                dense_loads(sp, r_, x1t, ROW, xd, agg, ROW, ad)

            @block.gpsimd
            def _(pool):
                def add_bias(n, s, u):
                    wait_alone(pool, r_["landed"][s], (u + 1) * 32)
                    if not (isinstance(u, int) and u == 0):
                        wait_alone(pool, r_["stored"][s], u * 16)
                    pool.tensor_tensor(t3(od[s][:, 0:ROWS * D], D), t3(xd[s][:, :], ROW)[:, :, 0:D],
                                       over_r(b2_b[:, :], ROWS), ALU.add).then_inc(xb_ready, 1)

                add_bias(0, 0, 0)
                add_bias(1, 1, 0)
                with pool.Fori(1, (CHUNKS - 1) // 2) as i:
                    add_bias(i * 2, 0, i)
                    add_bias(i * 2 + 1, 1, i)
                add_bias(CHUNKS - 1, 0, (CHUNKS - 1) // 2)

            @block.vector
            def _(dve):
                def center(n, s, u):
                    dve.wait_ge(r_["landed"][s], (u + 1) * 32)
                    rows = t3(xd[s][:, :], ROW)[:, :, 0:D]
                    m = nw[s][:, 4, 0:ROWS]
                    dve.reduce_sum(m, rows, AX_X)
                    dve.drain()
                    dve.tensor_scalar(m, m, -1.0 / D, None, ALU.mult)
                    dve.drain()
                    dve.tensor_tensor(xcd[s], rows, over_c(m, D), ALU.add).then_inc(r_["centered"], 1)

                def variance(n, s, u):
                    dve.wait_ge(r_["squared"], n + 1)
                    dve.reduce_sum(nw[s][:, 0, 0:ROWS], sqd[:, :, :], AX_X).then_inc(r_["var"], 1)

                def combine(n, s, u):
                    dve.wait_ge(r_["rstd"], n + 1)
                    rd, dis = nw[s][:, 3, 0:ROWS], t3(xd[s][:, :], ROW)[:, :, D]
                    dve.reciprocal(nw[s][:, 2, 0:ROWS], nw[s][:, 1, 0:ROWS])
                    dve.tensor_tensor(nw[s][:, 5, 0:ROWS], dis, dis, ALU.mult)
                    dve.drain()
                    dve.tensor_tensor(rd, nw[s][:, 2, 0:ROWS], nw[s][:, 5, 0:ROWS], ALU.mult)
                    dve.drain()
                    h = t3(hd[:, :], D)
                    dve.scalar_tensor_tensor(out=xcd[s], in0=xcd[s], scalar=0.0, in1=over_c(rd, D),
                                             op0=ALU.max, op1=ALU.mult)
                    dve.drain()
                    dve.tensor_tensor(h, xcd[s], t3(ad[s][:, :], ROW)[:, :, 0:D], ALU.add).then_inc(r_["z"], 1)

                def finish(n, s, u):
                    dve.wait_ge(y_psum, n + 1)
                    dve.wait_ge(xb_ready, n + 1)
                    dve.tensor_tensor(od[s][:, 0:ROWS * D], od[s][:, 0:ROWS * D], ps_z[:, :], ALU.add)\
                        .then_inc(r_["made"][s], 1)
                    dve.drain().then_inc(r_["free"][s], 1)
                    dve.drain().then_inc(r_["gl_free"], 1)

                for s in range(2):
                    dve.sem_inc(r_["free"][s], 1)
                dve.sem_inc(r_["gl_free"], 1)
                center(0, 0, 0)
                variance(0, 0, 0)
                with dve.Fori(0, (CHUNKS - 1) // 2) as i:
                    combine(i * 2, 0, i)
                    center(i * 2 + 1, 1, i)
                    variance(i * 2 + 1, 1, i)
                    finish(i * 2, 0, i)
                    combine(i * 2 + 1, 1, i)
                    center(i * 2 + 2, 0, i + 1)
                    variance(i * 2 + 2, 0, i + 1)
                    finish(i * 2 + 1, 1, i)
                combine(CHUNKS - 1, 0, (CHUNKS - 1) // 2)
                finish(CHUNKS - 1, 0, (CHUNKS - 1) // 2)

            @block.tensor
            def _(pe):
                def project(n, s, u):
                    pe.wait_ge(r_["z"], n + 1)
                    for j in range(ROWS // 2):
                        last = pe.transpose(ps_t[:, j * P:(j + 1) * P], hd[:, j * P:(j + 1) * P], ident[:, :])
                    last.then_inc(s_psum, 1)
                    pe.wait_ge(sT_ready, n + 1)
                    pe.wait_ge(r_["gl_free"], n + 1)
                    for j in range(ROWS // 2):
                        last = pe.matmul(ps_z[:, j * P:(j + 1) * P], gl_flat[:, j * P:(j + 1) * P], w_2[:, :],
                                         start=True, stop=True)
                    last.then_inc(y_psum, 1)

                project(0, 0, 0)
                over_chunks(pe, project)

            @block.scalar
            def _(act):
                def square(n, s, u):
                    act.wait_ge(r_["centered"], n + 1)
                    act.activation(sqd[:, :, :], xcd[s], ACT.Square).then_inc(r_["squared"], 1)
                    act.wait_ge(r_["var"], n + 1)
                    act.activation(nw[s][:, 1, 0:ROWS], nw[s][:, 0, 0:ROWS], ACT.Sqrt, bias=eps[:, :],
                                   scale=1.0 / D).then_inc(r_["rstd"], 1)

                def evict(n, s, u):
                    act.wait_ge(s_psum, n + 1)
                    act.activation(gl_flat[:, :], ps_t[:, :], ACT.Copy).then_inc(sT_ready, 1)

                def store(n, s, u):
                    act.wait_ge(r_["made"][s], u + 1)
                    act.dma_start(chunk_at(out, D, n), od[s][:, 0:ROWS * D]).then_inc(r_["stored"][s], 16)

                half = (CHUNKS - 1) // 2
                square(0, 0, 0)
                evict(0, 0, 0)
                square(1, 1, 0)
                store(0, 0, 0)
                with act.Fori(1, half) as i:
                    evict(i * 2 - 1, 1, i - 1)
                    square(i * 2, 0, i)
                    store(i * 2 - 1, 1, i - 1)
                    evict(i * 2, 0, i)
                    square(i * 2 + 1, 1, i)
                    store(i * 2, 0, i)
                evict(CHUNKS - 2, 1, half - 1)
                square(CHUNKS - 1, 0, half)
                store(CHUNKS - 2, 1, half - 1)
                evict(CHUNKS - 1, 0, half)
                act.wait_ge(r_["stored"][1], 16 * half)
                store(CHUNKS - 1, 0, half)
                act.wait_ge(r_["stored"][0], 16 * (half + 1))


_INS = ["x", "src", "dst", "edge_attr_16", "L0_gnn_W_l", "L0_gnn_b_l", "L0_gnn_W_r", "L0_gnn_b_r", "L0_gnn_W_e",
        "L0_gnn_att", "L0_gnn_bias", "L0_gnn_gamma", "L0_gnn_beta", "L1_gnn_W", "L1_gnn_b"]


def kernel(**inputs):
    import numpy as np
    import concourse.bacc as bacc
    from concourse.bass_utils import run_bass_kernel_spmd

    arrays = {name: np.ascontiguousarray(inputs[name]) for name in _INS}
    pad = EP - E
    arrays["src"] = np.concatenate([arrays["src"], np.zeros(pad, np.int32)])
    arrays["dst"] = np.concatenate([np.full(1, -1, np.int32), arrays["dst"], np.full(pad + 1, N, np.int32)])
    arrays["edge_attr_16"] = np.concatenate([arrays["edge_attr_16"], np.zeros((pad, ED), np.float32)])

    nc = bacc.Bacc("TRN2", target_bir_lowering=False, num_devices=1)
    aps = [nc.dram_tensor(f"in_{n}", arrays[n].shape, mybir.dt.from_np(arrays[n].dtype), kind="ExternalInput").ap()
           for n in _INS]
    agg = nc.dram_tensor("agg", (NT, ROW), F32, kind="Internal").ap()
    x1t = nc.dram_tensor("x1t", (N, ROW), F32, kind="Internal").ap()
    out = nc.dram_tensor("out_x", (N, D), F32, kind="ExternalOutput").ap()
    build(nc, *aps, agg, x1t, out)
    r = run_bass_kernel_spmd(nc, [{f"in_{n}": arrays[n] for n in _INS}], core_ids=[0])
    return r.results[0]["out_x"]
```

```python
from contextlib import ExitStack

import concourse.bass as bass
from concourse import mybir

F32 = mybir.dt.float32
I32 = mybir.dt.int32
U32 = mybir.dt.uint32
ALU = mybir.AluOpType
ACT = mybir.ActivationFunctionType
AX_X = mybir.AxisListType.X

P = 128
N = 100000
E = 50000
D = 64
ED = 16
H = 4
C = D // H
TILES = 49
BLOCKS = -(-E // (P * TILES))
EP = BLOCKS * P * TILES
GROUP = 7
GROUPS = TILES // GROUP
ALLT = BLOCKS * TILES
CNT = D
DEN = D + 1
REC = D + 1 + H
ROW = D + 1
ROWS = 24
CHUNK = P * ROWS
CHUNKS = -(-N // CHUNK)
ZROWS = -(-N // (P * BLOCKS * GROUPS))
NT = P * ZROWS * BLOCKS * GROUPS
BIG = 1.0e30
SKIP = float(1 << 20)
LN_EPS = 1e-5
BN_EPS = 1e-5
SLOPE = 0.2
RSQRT_MAGIC = float(0x5F3759DF)


def build(nc, x, src, dst, ea, W_l, b_l, W_r, b_r, W_e, att, bias, gamma, beta, W2, b2, agg, x1t, out):
    ctx = ExitStack()
    with ctx:
        def sb(name, shape, dt=F32):
            return ctx.enter_context(nc.sbuf_tensor(name, shape, dt))

        def psum(name, shape):
            return ctx.enter_context(nc.psum_tensor(name, shape, F32))

        def sem(name):
            return ctx.enter_context(nc.semaphore(name))

        waits_passed = sem("waits_passed")

        def wait_alone(eng, signal, count):
            eng.wait_ge(signal, count)
            eng.sem_inc(waits_passed, 1)

        rec_flat = sb("rec", [P, ALLT * REC])
        rec = rec_flat[:, :].rearrange("p (t c) -> p t c", c=REC)
        src_i = sb("src_i", [P, ALLT + TILES], I32)
        row_i = sb("row_i", [P, ALLT], I32)
        dstg_i = sb("dstg_i", [P, ALLT + TILES], I32)
        same = sb("same", [P, ALLT])
        first = sb("first", [P, ALLT])
        pen = sb("pen", [P, 2, TILES])
        is_end = sb("is_end", [P, ALLT])
        dis_dst = sb("dis_dst", [P, ALLT])
        idx_stage = [sb(f"idx_stage{s}", [P, 2 * GROUP], I32) for s in range(GROUPS)]
        ident = sb("ident", [P, P])
        ones = sb("ones", [1, P])
        eps = sb("eps", [P, 1])
        w_h = sb("w_h", [P, 2 * D])
        w_ea = sb("w_ea", [GROUP * ED + 2, GROUP * 2 * D])
        w_2 = sb("w_2", [P, 2 * D])
        block_last = sb("block_last", [1, BLOCKS], I32)
        chunk_first = sb("chunk_first", [1, CHUNKS], I32)
        blocks_f = sb("blocks_f", [1, CHUNKS])
        blocks_needed = sb("blocks_needed", [1, CHUNKS], I32)
        att_b = sb("att_b", [P, D])
        b2_b = sb("b2_b", [P, D])
        bn_b = sb("bn_b", [P, D])
        b_rows = sb("b_rows", [1, 512])
        stat_sum = sb("stat_sum", [1, 2 * D])
        ea_in = [sb(f"ea_in{s}", [P, GROUP * ED + 2]) for s in range(2)]
        ea_t = sb("ea_t", [GROUP * ED + 2, P])
        stats = sb("stats", [P, 2 * GROUP, 6])
        small = sb("small", [P, 8, 2 * GROUP])
        pk = sb("pk", [P, 2, REC])
        pm = sb("pm", [P, 2, H])
        row_m = sb("row_m", [H, 2 * P])
        run_m = sb("run_m", [H, P + 1])
        row_v = sb("row_v", [REC, 2 * P])
        run_v = sb("run_v", [REC, P + 1])
        carry = sb("carry", [P, REC])
        statd = sb("statd", [P, ROWS, 6])
        nw = [sb(f"nw{s}", [P, 8, ROWS]) for s in range(2)]
        work = sb("work", [P, 8 * ROWS * ROW + 3 * ROWS * D])

        def pieces(sizes, at=0):
            views = []
            for n in sizes:
                views.append(work[:, at:at + n])
                at += n
            return views

        dense = pieces([ROWS * ROW] * 8 + [ROWS * D] * 3)
        xd, ad, od, hd, sT = dense[0:3], dense[3:6], dense[6:8], dense[8:10], dense[10]
        vecs, bn, bn_ab = (sT[0:1, a * D:b * D].rearrange("p (j c) -> p j c", c=D) for a, b in ((0, 3), (3, 11), (11, 13)))
        edge_sizes = [2 * GROUP * D] * (GROUPS + 2) + [GROUP * P, GROUP * D, TILES * D] + [TILES * H] * 5 + \
            [3 * TILES * H, H * (TILES + 1), TILES]
        edge = pieces(edge_sizes)
        zero = work[:, sum(edge_sizes):sum(edge_sizes) + ZROWS * ROW]
        dst_i, prev_i, next_i = (v.bitcast(I32) for v in pieces([ALLT] * 3))
        block_in = work[0:1, 3 * ALLT:3 * ALLT + CHUNKS * BLOCKS].rearrange("p (m k) -> p m k", k=BLOCKS)
        xg = edge[0:GROUPS]
        edge = edge[GROUPS - 3:]
        sq = edge[3].rearrange("p (t c) -> p t c", c=D)
        hn, hT = edge[4], edge[5]
        zs = edge[6].rearrange("p (t c) -> p t c", c=D)
        wide = edge[7]
        logit, rfac, ffac = (v.rearrange("p (h t) -> p h t", h=H) for v in edge[8:11])
        ffac_t, wide_d = (v.rearrange("p (t h) -> p t h", h=H) for v in edge[11:13])
        expo = edge[13].rearrange("p (j h t) -> p j h t", j=3, h=H)
        mx = edge[14].rearrange("p (h t) -> p h t", h=H)
        end_blk = edge[15]

        ps_t = psum("ps_t", [P, 1536])
        ps_z = psum("ps_z", [P, 1536])
        ps_e = psum("ps_e", [P, 512])
        ps_c = psum("ps_c", [P, 512])
        ps_o = [ps_t[0:1, 1024:1024 + D], ps_z[0:1, 1024:1024 + D]]

        def t3(ap, c):
            return ap.rearrange("p (t c) -> p t c", c=c)

        def rows_of(ap):
            return t3(ap, ROW)[:, :, 0:D]

        def over_c(ap, n):
            return ap.unsqueeze(len(ap.shape)).to_broadcast(list(ap.shape) + [n])

        def over_r(ap, n):
            return ap.unsqueeze(1).to_broadcast([ap.shape[0], n] + list(ap.shape[1:]))

        edges_in = sem("edges_in")
        weights_in = sem("weights_in")
        cleared = sem("cleared")
        ident_zero = sem("ident_zero")
        chunks_known = sem("chunks_known")
        agg_zeroed = sem("agg_zeroed")
        with nc.Block() as block:
            @block.sync
            def _(sp):
                def per_edge(ap):
                    return ap.rearrange("(k p t) -> p k t", p=P, t=TILES)

                def tile3(t):
                    return t[:, 0:ALLT].rearrange("p (k t) -> p k t", t=TILES)
                sp.dma_start(tile3(dst_i), per_edge(dst[1:1 + EP])).then_inc(edges_in, 16)
                sp.dma_start(tile3(prev_i), per_edge(dst[0:EP])).then_inc(edges_in, 16)
                sp.dma_start(tile3(next_i), per_edge(dst[2:2 + EP])).then_inc(edges_in, 16)
                sp.dma_start(tile3(src_i), per_edge(src)).then_inc(edges_in, 16)
                every = dst[1:1 + EP].rearrange("(k r) -> k r", r=P * TILES)
                sp.dma_start(block_last[:, :], every[:, P * TILES - 1:P * TILES].rearrange("k o -> o k"),
                             allow_slow_non_contiguous=True).then_inc(edges_in, 16)

            @block.scalar
            def _(act):
                act.wait_ge(cleared, 4)
                act.dma_start(w_h[0:D, 0:D], W_l).then_inc(weights_in, 16)
                act.dma_start(w_h[0:D, D:2 * D], W_l).then_inc(weights_in, 16)
                act.dma_start(w_h[D:2 * D, D:2 * D], W_r).then_inc(weights_in, 16)
                for j in range(GROUP):
                    act.dma_start(w_ea[j * ED:(j + 1) * ED, j * 2 * D + D:(j + 1) * 2 * D], W_e).then_inc(weights_in, 16)
                k0 = GROUP * ED
                for j in range(GROUP):
                    act.dma_start(w_ea[k0:k0 + 1, j * 2 * D:j * 2 * D + D], b_l.unsqueeze(0)).then_inc(weights_in, 16)
                    act.dma_start(w_ea[k0:k0 + 1, j * 2 * D + D:(j + 1) * 2 * D], b_l.unsqueeze(0)).then_inc(weights_in, 16)
                    act.dma_start(w_ea[k0 + 1:k0 + 2, j * 2 * D + D:(j + 1) * 2 * D], b_r.unsqueeze(0)).then_inc(weights_in, 16)
                act.dma_start(w_2[0:D, 0:D], W2).then_inc(weights_in, 16)
                act.dma_start(w_2[D:2 * D, D:2 * D], W2).then_inc(weights_in, 16)
                act.dma_start(att_b[:, :], att.rearrange("h c -> (h c)").partition_broadcast(P)).then_inc(weights_in, 16)
                act.dma_start(b2_b[:, :], b2.partition_broadcast(P)).then_inc(weights_in, 16)
                act.wait_ge(weights_in, 16 * (3 + GROUP + 3 * GROUP + 4))

            @block.gpsimd
            def _(pool):
                pool.memset(ident[:, :], 0.0).then_inc(ident_zero, 1)
                pool.wait_ge(ident_zero, 1)
                pool.affine_select(out=ident[:, :], in_=ident[:, :], compare_op=ALU.not_equal, fill=1.0,
                                   base=0, pattern=[[-1, P]], channel_multiplier=1).then_inc(ident_zero, 1)
                pool.iota(chunk_first[:, :], pattern=[[-CHUNK, CHUNKS]], base=(CHUNKS - 1) * CHUNK,
                          channel_multiplier=0).then_inc(chunks_known, 1)
                pool.wait_ge(chunks_known, 1)
                pool.memset(chunk_first[:, 0:1], N - CHUNK).then_inc(chunks_known, 1)
                pool.wait_ge(ident_zero, 2)

            @block.vector
            def _(dve):
                dve.memset(zero, 0.0).then_inc(cleared, 1)
                dve.memset(w_h[:, :], 0.0).then_inc(cleared, 1)
                dve.memset(w_ea[:, :], 0.0).then_inc(cleared, 1)
                dve.memset(w_2[:, :], 0.0).then_inc(cleared, 1)
                dve.memset(ones[:, :], 1.0)
                dve.memset(eps[:, :], LN_EPS)
                dve.memset(stat_sum[:, :], 0.0)
                dve.memset(run_m[:, :], -BIG)
                dve.memset(run_v[:, :], 0.0)
                for s in range(2):
                    dve.memset(ea_in[s][:, GROUP * ED:GROUP * ED + 2], 1.0)
                dve.memset(src_i[:, ALLT:ALLT + TILES], 0)
                dve.memset(dstg_i[:, ALLT:ALLT + TILES], 0)
                dve.wait_ge(edges_in, 80)
                dve.wait_ge(chunks_known, 2)
                dve.tensor_tensor(same[:, :], dst_i[:, :], prev_i[:, :], ALU.is_equal)
                dve.tensor_tensor(is_end[:, :], dst_i[:, :], next_i[:, :], ALU.not_equal)
                dve.tensor_tensor(block_in, over_r(block_last[:, :], CHUNKS),
                                  over_c(chunk_first[:, :], BLOCKS), ALU.is_ge)
                before = t3(prev_i[:, :], TILES)[:, :, 0]
                dve.tensor_tensor(t3(first[:, :], TILES), t3(dst_i[:, :], TILES), over_c(before, TILES), ALU.is_equal)
                dve.tensor_scalar(dstg_i[:, 0:ALLT], dst_i[:, :], float(N - 1), None, ALU.min)
                dve.drain()
                dve.reduce_sum(blocks_f[:, :], block_in, AX_X)
                dve.tensor_scalar(dis_dst[:, :], is_end[:, :], -SKIP, SKIP, ALU.mult, ALU.add)
                dve.drain()
                dve.tensor_copy(blocks_needed[:, :], blocks_f[:, :])
                dve.tensor_tensor(row_i[:, :], dst_i[:, :], dis_dst[:, :], ALU.add)
                dve.drain()

        def slot_use(k, g):
            return k * (GROUPS - GROUPS // 2) + g // 2 if g % 2 == 0 else k * (GROUPS // 2) + g // 2

        def norm_sums(dve, st, out, n):
            half = D // 2
            dve.tensor_tensor(out[:, 0, 0:n], st[:, 0:n, 1], st[:, 0:n, 4], ALU.add)
            dve.tensor_tensor(out[:, 1, 0:n], st[:, 0:n, 1], st[:, 0:n, 4], ALU.subtract)
            dve.tensor_tensor(out[:, 6, 0:n], st[:, 0:n, 2], st[:, 0:n, 5], ALU.add)
            dve.drain()
            dve.tensor_tensor(out[:, 1, 0:n], out[:, 1, 0:n], out[:, 1, 0:n], ALU.mult)
            dve.drain()
            return dve.scalar_tensor_tensor(out=out[:, 2, 0:n], in0=out[:, 1, 0:n], scalar=half / 2.0,
                                            in1=out[:, 6, 0:n], op0=ALU.mult, op1=ALU.add)

        def scan_over_partitions(dve, row, run, n, op0, op1, ps):
            dve.tensor_copy(row[0:n, :], ps[0:n, 0:2 * P])
            dve.tensor_copy(run[0:n, 0:1], run[0:n, P:P + 1])
            dve.drain()
            return dve.tensor_tensor_scan(run[0:n, 1:P + 1], row[0:n, P:2 * P], row[0:n, 0:P], run[0:n, 0:1], op0, op1)

        idx_staged = sem("idx_staged")
        gathered = [sem(f"gathered{s}") for s in range(GROUPS)]
        xg_free = [sem(f"xg_free{s}") for s in range(GROUPS)]
        ea_landed = [sem(f"ea_landed{s}") for s in range(2)]
        ea_turned = [sem(f"ea_turned{s}") for s in range(2)]
        var_ready = sem("var_ready")
        std_ready = sem("std_ready")
        scale_ready = sem("scale_ready")
        h_ready = sem("h_ready")
        hT_psum = sem("hT_psum")
        hT_ready = sem("hT_ready")
        ea_t_ready = sem("ea_t_ready")
        z_psum = sem("z_psum")
        z_ready = sem("z_ready")
        zs_free = sem("zs_free")
        max_rows = sem("max_rows")
        max_rows_t = sem("max_rows_t")
        max_run = sem("max_run")
        max_carry = sem("max_carry")
        expo_in = sem("expo_in")
        expo_out = sem("expo_out")
        sum_rows = sem("sum_rows")
        sum_rows_t = sem("sum_rows_t")
        sum_run = sem("sum_run")
        sum_carry = sem("sum_carry")
        o_ready = sem("o_ready")
        o_squared = sem("o_squared")
        stats_psum = sem("stats_psum")
        with nc.Block() as block:
            @block.sync
            def _(sp):
                ea_r = ea.rearrange("(k p t) c -> k p (t c)", p=P, t=TILES)
                with sp.Fori(0, BLOCKS) as k:
                    for g in range(GROUPS):
                        s, use = g % 2, slot_use(k, g)
                        sp.wait_ge(ea_turned[s], use + 1)
                        sp.dma_start(ea_in[s][:, 0:GROUP * ED],
                                     ea_r[bass.ds(k, 1), :, g * GROUP * ED:(g + 1) * GROUP * ED]
                                     .rearrange("k p c -> p (k c)")).then_inc(ea_landed[s], 16)
                        sp.dma_start(agg[bass.ds((k * GROUPS + g) * (P * ZROWS), P * ZROWS), :]
                                     .rearrange("(p r) c -> p (r c)", p=P), zero).then_inc(agg_zeroed, 16)
                sp.wait_ge(agg_zeroed, 16 * BLOCKS * GROUPS)

            @block.gpsimd
            def _(pool):
                with pool.Fori(0, BLOCKS) as k:
                    for g in range(GROUPS):
                        s = g
                        wait_alone(pool, idx_staged, k * GROUPS + (g + 1))
                        wait_alone(pool, xg_free[g], k + 1)
                        for t in range(GROUP):
                            for side in range(2):
                                a = (2 * t + side) * D
                                i = side * GROUP + t
                                pool.indirect_dma_start(
                                    xg[s][:, a:a + D], None, x,
                                    bass.IndirectOffsetOnAxis(ap=idx_stage[s][:, i:i + 1].bitcast(U32), axis=0),
                                    bounds_check=N - 1, oob_is_err=False).then_inc(gathered[s], 16)

            @block.scalar
            def _(act):
                def normalize(k, g):
                    s, n = g, k * GROUPS + (g + 1)
                    act.wait_ge(var_ready, n)
                    act.activation(small[:, 3, :], small[:, 2, :], ACT.Sqrt, bias=eps[:, :],
                                   scale=1.0 / D).then_inc(std_ready, 1)
                    act.wait_ge(scale_ready, n)
                    act.wait_ge(hT_psum, n)
                    for r in range(2 * GROUP):
                        last = act.activation(hn[:, r * D:(r + 1) * D], xg[s][:, r * D:(r + 1) * D], ACT.Relu,
                                              bias=small[:, 5, r:r + 1], scale=small[:, 4, r:r + 1])
                    last.then_inc(h_ready, 1)
                    act.drain().then_inc(xg_free[s], 1)

                def take_z(k, g):
                    n = k * GROUPS + (g + 1)
                    wait_alone(act, z_psum, n)
                    z = t3(ps_z[:, 0:GROUP * 2 * D], 2 * D)
                    act.activation(rec[:, bass.ds(k * TILES + g * GROUP, GROUP), 0:D], z[:, :, 0:D], ACT.Copy)
                    act.wait_ge(zs_free, n)
                    act.activation(zs, z[:, :, D:2 * D], ACT.Copy).then_inc(z_ready, 1)

                def take_turned(k, g):
                    s, use, n = g % 2, slot_use(k, g), k * GROUPS + (g + 1)
                    act.wait_ge(ea_turned[s], use + 2)
                    act.activation(ea_t[:, :], ps_e[0:GROUP * ED + 2, 0:P], ACT.Copy).then_inc(ea_t_ready, 1)
                    act.wait_ge(hT_psum, n + 1)
                    act.activation(hT, ps_t[:, 0:GROUP * P], ACT.Copy).then_inc(hT_ready, 1)

                with act.Fori(0, BLOCKS) as k:
                    for g in range(GROUPS):
                        normalize(k, g)
                        if g:
                            take_z(k, g - 1)
                        take_turned(k, g)
                    take_z(k, GROUPS - 1)
                    act.wait_ge(expo_in, k + 1)
                    act.activation(expo, expo, ACT.Exp).then_inc(expo_out, 1)
                    wait_alone(act, o_ready, k + 1)
                    act.activation(t3(wide, D), rec[:, bass.ds(k * TILES, TILES), 0:D], ACT.Square).then_inc(o_squared, 1)

            @block.tensor
            def _(pe):
                for s in range(2):
                    pe.sem_inc(ea_turned[s], 1)
                pe.sem_inc(hT_psum, 1)
                with pe.Fori(0, BLOCKS) as k:
                    for g in range(GROUPS):
                        s, use, n = g % 2, slot_use(k, g), k * GROUPS + (g + 1)
                        pe.wait_ge(ea_landed[s], (use + 1) * 16)
                        pe.transpose(ps_e[0:GROUP * ED + 2, 0:P], ea_in[s][:, :], ident[:, :]).then_inc(ea_turned[s], 1)
                        pe.wait_ge(h_ready, n)
                        for t in range(GROUP):
                            last = pe.transpose(ps_t[:, t * P:(t + 1) * P], hn[:, t * P:(t + 1) * P], ident[:, :])
                        last.then_inc(hT_psum, 1)
                        pe.wait_ge(ea_t_ready, n)
                        pe.wait_ge(z_ready, n)
                        for a, b in ((0, 4), (4, GROUP)):
                            pe.matmul(ps_z[:, a * P:b * P], ea_t[:, :], w_ea[:, a * P:b * P], start=True, stop=False,
                                      skip_group_check=True)
                        pe.wait_ge(hT_ready, n)
                        for t in range(GROUP):
                            last = pe.matmul(ps_z[:, t * P:(t + 1) * P], hT[:, t * P:(t + 1) * P], w_h[:, :],
                                             start=False, stop=True, skip_group_check=True)
                        last.then_inc(z_psum, 1)
                    wait_alone(pe, max_rows, k + 1)
                    for j in range(2):
                        last = pe.transpose(ps_c[0:H, j * P:(j + 1) * P], pm[:, j, :], ident[:, :])
                    last.then_inc(max_rows_t, 1)
                    wait_alone(pe, max_run, k + 1)
                    pe.transpose(ps_e[:, 0:H], run_m[:, 0:P], ident[0:H, 0:H]).then_inc(max_carry, 1)
                    wait_alone(pe, sum_rows, k + 1)
                    for j in range(2):
                        last = pe.transpose(ps_c[0:REC, j * P:(j + 1) * P], pk[:, j, :], ident[:, :])
                    last.then_inc(sum_rows_t, 1)
                    wait_alone(pe, sum_run, k + 1)
                    pe.transpose(ps_e[:, 0:REC], run_v[:, 0:P], ident[0:REC, 0:REC]).then_inc(sum_carry, 1)
                    pe.wait_ge(o_squared, k + 1)
                    for j in range(2):
                        for t in range(TILES):
                            rhs = rec[:, bass.ds(k * TILES + t, 1), 0:D].rearrange("p t c -> p (t c)") if j == 0 else \
                                wide[:, t * D:(t + 1) * D]
                            last = pe.matmul(ps_o[j], end_blk[:, t:t + 1], rhs,
                                             start=(t == 0), stop=(t == TILES - 1))
                    last.then_inc(stats_psum, 1)

            @block.vector
            def _(dve):
                def stage_indices(k, g):
                    a = k * TILES + g * GROUP
                    dve.tensor_copy(idx_stage[g][:, 0:GROUP], src_i[:, bass.ds(a, GROUP)])
                    dve.tensor_copy(idx_stage[g][:, GROUP:2 * GROUP], dstg_i[:, bass.ds(a, GROUP)]).then_inc(idx_staged, 1)

                def layer_norm(k, g):
                    s, n = g, k * GROUPS + (g + 1)
                    dve.wait_ge(gathered[g], (k + 1) * (2 * GROUP * 16))
                    stage_indices(k + 1, g)
                    for r in range(2 * GROUP):
                        dve.bn_stats(stats[:, r, :], xg[s][:, r * D:(r + 1) * D])
                    dve.drain()
                    norm_sums(dve, stats, small, 2 * GROUP).then_inc(var_ready, 1)
                    dve.wait_ge(std_ready, n)
                    dve.reciprocal(small[:, 4, :], small[:, 3, :])
                    dve.drain()
                    dve.scalar_tensor_tensor(out=small[:, 5, :], in0=small[:, 0, :], scalar=-0.5, in1=small[:, 4, :],
                                             op0=ALU.mult, op1=ALU.mult).then_inc(scale_ready, 1)

                def logits(k, g):
                    n = k * GROUPS + (g + 1)
                    dve.wait_ge(z_ready, n + 1)
                    dve.scalar_tensor_tensor(out=sq[:, 0:GROUP, :], in0=zs, scalar=SLOPE, in1=zs,
                                             op0=ALU.mult, op1=ALU.max)
                    dve.drain().then_inc(zs_free, 1)
                    dve.tensor_tensor(sq[:, GROUP:2 * GROUP, :], sq[:, 0:GROUP, :], over_r(att_b[:, :], GROUP), ALU.mult)
                    dve.drain()
                    dve.reduce_sum(logit[:, :, g * GROUP:(g + 1) * GROUP].rearrange("p h t -> p t h"),
                                   sq[:, GROUP:2 * GROUP, :].rearrange("p t (h c) -> p t h c", h=H), AX_X)
                    dve.drain()

                for g in range(GROUPS):
                    dve.sem_inc(xg_free[g], 1)
                    stage_indices(0, g)
                dve.sem_inc(zs_free, 1)
                dve.sem_inc(z_ready, 1)
                with dve.Fori(0, BLOCKS) as k:
                    blk = bass.ds(k * TILES, TILES)
                    for g in range(GROUPS):
                        layer_norm(k, g)
                        if g:
                            logits(k, g - 1)
                    logits(k, GROUPS - 1)
                    dve.tensor_scalar(pen[:, 0, :], same[:, blk], -1.0, BIG, ALU.add, ALU.mult)
                    dve.tensor_scalar(pen[:, 1, :], first[:, blk], -1.0, BIG, ALU.add, ALU.mult)
                    dve.drain()
                    for h in range(H):
                        dve.tensor_tensor_scan(mx[:, h, 1:TILES + 1], pen[:, 0, :], logit[:, h, :], -BIG,
                                               ALU.add, ALU.max)
                    dve.drain()
                    dve.tensor_copy(pm[:, 0, :], mx[:, :, TILES])
                    dve.tensor_copy(pm[:, 1, :], pen[:, 1, TILES - 1:TILES].to_broadcast([P, H]))\
                        .then_inc(max_rows, 1)
                    dve.wait_ge(max_rows_t, k + 1)
                    scan_over_partitions(dve, row_m, run_m, H, ALU.add, ALU.max, ps_c).then_inc(max_run, 1)
                    dve.wait_ge(max_carry, k + 1)
                    dve.tensor_copy(mx[:, :, 0], ps_e[:, 0:H])
                    dve.drain()
                    came = over_c(mx[:, :, 0], TILES)
                    dve.tensor_tensor(rfac[:, :, :], came, over_r(pen[:, 1, :], H), ALU.add)
                    dve.drain()
                    dve.tensor_tensor(mx[:, :, 1:TILES + 1], mx[:, :, 1:TILES + 1], rfac[:, :, :], ALU.max)
                    dve.drain()
                    now = mx[:, :, 1:TILES + 1]
                    dve.tensor_tensor(expo[:, 0, :, :], mx[:, :, 0:TILES], now, ALU.subtract)
                    dve.tensor_tensor(expo[:, 1, :, :], came, now, ALU.subtract)
                    dve.tensor_tensor(expo[:, 2, :, :], logit, now, ALU.subtract)
                    dve.drain()
                    dve.tensor_scalar(expo, expo, 0.0, None, ALU.min).then_inc(expo_in, 1)
                    dve.wait_ge(expo_out, k + 1)
                    dve.tensor_tensor(rfac[:, :, :], expo[:, 0, :, :], over_r(same[:, blk], H), ALU.mult)
                    dve.tensor_tensor(ffac[:, :, :], expo[:, 1, :, :], over_r(first[:, blk], H), ALU.mult)
                    ex_t = expo[:, 2, :, :].rearrange("p h t -> p t h")
                    heads = rec[:, blk, 0:D].rearrange("p t (h c) -> p t h c", h=H)
                    dve.tensor_tensor(heads, heads, over_c(ex_t, C), ALU.mult)
                    dve.tensor_copy(rec[:, blk, DEN:DEN + H], ex_t)
                    dve.tensor_scalar(rec[:, blk, CNT], same[:, blk], 0.0, 1.0, ALU.mult, ALU.add)
                    dve.tensor_copy(end_blk[:, :], is_end[:, blk])
                    dve.drain()
                    for c in range(REC):
                        decay = same[:, blk] if c == CNT else rfac[:, c // C if c < D else c - DEN, :]
                        col = rec[:, blk, c]
                        dve.tensor_tensor_scan(col, decay, col, 0.0, ALU.mult, ALU.add)
                    dve.drain()
                    at_end = bass.ds(k * TILES + TILES - 1, 1)
                    dve.tensor_copy(pk[:, 0, :], rec[:, at_end, :].rearrange("p t c -> p (t c)"))
                    last = ffac[:, :, TILES - 1]
                    dve.tensor_copy(pk[:, 1, 0:D].rearrange("p (h c) -> p h c", h=H), over_c(last, C))
                    dve.tensor_copy(pk[:, 1, DEN:DEN + H], last)
                    dve.tensor_copy(pk[:, 1, CNT:CNT + 1], first[:, at_end])
                    dve.tensor_copy(ffac_t[:, :, :], ffac[:, :, :].rearrange("p h t -> p t h"))
                    dve.drain().then_inc(sum_rows, 1)
                    dve.wait_ge(sum_rows_t, k + 1)
                    scan_over_partitions(dve, row_v, run_v, REC, ALU.mult, ALU.add, ps_c).then_inc(sum_run, 1)
                    dve.wait_ge(sum_carry, k + 1)
                    dve.tensor_copy(carry[:, :], ps_e[:, 0:REC])
                    dve.drain()
                    w4 = wide.rearrange("p (t h c) -> p t h c", h=H, c=C)
                    dve.tensor_tensor(w4, over_c(ffac_t[:, :, :], C),
                                      over_r(carry[:, 0:D].rearrange("p (h c) -> p h c", h=H), TILES), ALU.mult)
                    dve.tensor_tensor(wide_d[:, :, :], ffac_t[:, :, :], over_r(carry[:, DEN:DEN + H], TILES), ALU.mult)
                    dve.scalar_tensor_tensor(out=rec[:, blk, CNT], in0=first[:, blk], scalar=carry[:, CNT:CNT + 1],
                                             in1=rec[:, blk, CNT], op0=ALU.mult, op1=ALU.add)
                    dve.drain()
                    dve.tensor_tensor(rec[:, blk, 0:D], rec[:, blk, 0:D], t3(wide, D), ALU.add)
                    dve.scalar_tensor_tensor(out=wide_d[:, :, :], in0=wide_d[:, :, :], scalar=1e-16,
                                             in1=rec[:, blk, DEN:DEN + H], op0=ALU.add, op1=ALU.add)
                    dve.drain()
                    dve.reciprocal(wide_d[:, :, :], wide_d[:, :, :])
                    dve.drain()
                    dve.tensor_tensor(heads, heads, over_c(wide_d[:, :, :], C), ALU.mult).then_inc(o_ready, 1)
                    dve.wait_ge(stats_psum, k + 1)
                    for j in range(2):
                        part = stat_sum[:, j * D:(j + 1) * D]
                        dve.tensor_tensor(part, part, ps_o[j], ALU.add)
                    dve.drain()

        def chunk_at(ap, w, m):
            start = N - CHUNK if isinstance(m, int) and m == 0 else (CHUNKS - 1 - m) * CHUNK if isinstance(m, int) \
                else (CHUNKS - 1) * CHUNK - m * CHUNK
            return ap[bass.ds(start, CHUNK), :].rearrange("(p r) c -> p (r c)", p=P)

        def over_chunks(eng, step):
            def fixed(m):
                def at(lag):
                    c = m - lag
                    return (c, c % 2, c // 2, c % 3, c // 3) if 0 <= c < CHUNKS else None
                return at

            def looped(i, j):
                def at(lag):
                    c = j - lag
                    return (i * 6 + c, c % 2, i * 3 + c // 2, c % 3, i * 2 + c // 3)
                return at
            for m in range(3):
                step(fixed(m))
            assert (CHUNKS - 3) % 6 == 0
            with eng.Fori(0, (CHUNKS - 3) // 6) as i:
                for j in range(3, 9):
                    step(looped(i, j))
            for m in range(CHUNKS, CHUNKS + 2):
                step(fixed(m))

        def first_use(u):
            return isinstance(u, int) and u == 0

        def dense_sems(tag):
            return {n: [sem(f"{tag}_{n}{s}") for s in range(slots)]
                    for n, slots in (("landed", 3), ("free", 3), ("made", 2), ("stored", 2))}

        def dense_loads(sp, q, table, w, tiles, stored_blocks):
            def load(at):
                if at(0):
                    m, _, _, s, u = at(0)
                    sp.wait_ge(q["free"][s], u + 1)
                    sp.dma_start(tiles[s][:, 0:ROWS * w], chunk_at(table, w, m)).then_inc(q["landed"][s], 16)
                    sp.wait_ge(stored_blocks, sp.value_load(blocks_needed[0:1, bass.ds(m, 1)], min_val=1, max_val=BLOCKS))
                    sp.dma_start(ad[s], chunk_at(agg, ROW, m)).then_inc(q["landed"][s], 16)
            over_chunks(sp, load)

        def dense_store(eng, q, table, w, chunk):
            m, s, u, _, _ = chunk
            eng.wait_ge(q["made"][s], u + 1)
            eng.dma_start(chunk_at(table, w, m), od[s][:, 0:ROWS * w]).then_inc(q["stored"][s], 16)
            if first_use(u) and s == 0:
                eng.wait_ge(q["stored"][0], 16)

        def scatter_blocks(pool, stored, stored_blocks, block_ready=None):
            def finished(j):
                pool.wait_ge(stored[j % 2], 16 * TILES * (j // 2 + 1))
                pool.sem_inc(stored_blocks, 1)
            for j, k in enumerate(range(BLOCKS - 1, -1, -1)):
                if block_ready is not None:
                    pool.wait_ge(block_ready, j + 1)
                for t in range(TILES):
                    a = k * TILES + t
                    pool.indirect_dma_start(
                        agg, bass.IndirectOffsetOnAxis(ap=row_i[:, a:a + 1].bitcast(U32), axis=0),
                        rec[:, a, 0:ROW], None, bounds_check=N - 1, oob_is_err=False).then_inc(stored[j % 2], 16)
                    if j and t == 2:
                        finished(j - 1)
            finished(BLOCKS - 1)

        def row_stats(dve, tile, w, s):
            for r in range(ROWS):
                dve.bn_stats(statd[:, r, :], tile[:, r * w:r * w + D])
            dve.drain()
            return norm_sums(dve, statd, nw[s], ROWS)

        def normalize_rows(act, tile, w, s, rows):
            for r in rows:
                last = act.activation(hd[s][:, r * D:(r + 1) * D], tile[:, r * w:r * w + D], ACT.Relu,
                                      bias=nw[s][:, 5, r:r + 1], scale=nw[s][:, 4, r:r + 1])
            return last

        cnt_std = sem("cnt_std")
        bn_var = sem("bn_var")
        bn_std = sem("bn_std")
        bn_row = sem("bn_row")
        bn_psum = sem("bn_psum")
        o_stored = [sem(f"o_stored{j}") for j in range(2)]
        o_blocks = sem("o_blocks")
        o_scaled = sem("o_scaled")
        vecs_in = sem("vecs_in")
        vecs_copied = sem("vecs_copied")
        x1_sum = sem("x1_sum")
        x1_scale = sem("x1_scale")
        x1_h = sem("x1_h")
        x1_z = sem("x1_z")
        x1_gelu = sem("x1_gelu")
        q = dense_sems("x1")
        with nc.Block() as block:
            @block.gpsimd
            def _(pool):
                scatter_blocks(pool, o_stored, o_blocks, o_scaled)

            @block.sync
            def _(sp):
                for j, v in enumerate((bias, gamma, beta)):
                    sp.dma_start(vecs[:, j, :], v.unsqueeze(0)).then_inc(vecs_in, 16)
                dense_loads(sp, q, x, D, xd, o_blocks)

            @block.tensor
            def _(pe):
                pe.wait_ge(bn_row, 1)
                pe.matmul(ps_c[:, 0:2 * D], ones[:, :], bn_ab[:, :, :].rearrange("p j c -> p (j c)"),
                          start=True, stop=True).then_inc(bn_psum, 1)
                pe.wait_ge(vecs_copied, 1)

                def step(at):
                    if at(0):
                        m, s, _, _, _ = at(0)
                        pe.wait_ge(x1_gelu, m + 1)
                        for j in range(ROWS * D // 512):
                            pe.matmul(ps_z[:, j * 512:(j + 1) * 512], ones[:, :], b_rows[:, :], start=True, stop=False)
                        pe.wait_ge(x1_z, m + 1)
                        for j in range(ROWS * D // 512):
                            last = pe.matmul(ps_z[:, j * 512:(j + 1) * 512], ident[:, :], hd[s][:, j * 512:(j + 1) * 512],
                                             start=False, stop=True)
                        last.then_inc(x1_sum, 1)
                over_chunks(pe, step)

            @block.scalar
            def _(act):
                act.sem_inc(x1_gelu, 1)
                act.wait_ge(bn_var, 1)
                act.activation(bn[:, 4, :], bn[:, 1, :], ACT.Sqrt, bias=eps[0:1, :], scale=1.0).then_inc(bn_std, 1)
                act.activation(dis_dst[:, :], rec[:, :, CNT], ACT.Copy, bias=1.0, scale=1.0)
                act.drain()
                act.activation(dis_dst[:, :], dis_dst[:, :], ACT.Sqrt).then_inc(cnt_std, 1)

                def step(at):
                    if at(0):
                        m, s, _, s3, _ = at(0)
                        act.wait_ge(x1_scale, m + 1)
                        normalize_rows(act, xd[s3], D, s, range(0, ROWS // 2))
                    if at(1):
                        m, s, _, _, _ = at(1)
                        act.wait_ge(x1_sum, m + 1)
                        act.activation(hd[s], ps_z[:, :], ACT.Gelu).then_inc(x1_gelu, 1)
                    if at(0):
                        m, s, _, s3, _ = at(0)
                        normalize_rows(act, xd[s3], D, s, range(ROWS // 2, ROWS)).then_inc(x1_h, 1)
                    if at(2):
                        dense_store(act, q, x1t, ROW, at(2))
                over_chunks(act, step)
                for s in range(2):
                    act.wait_ge(q["stored"][s], 16 * ((CHUNKS + 1 - s) // 2))

            @block.vector
            def _(dve):
                mean, var, sq_m, rstd = (bn[:, j, :] for j in range(4))
                dve.tensor_scalar(mean, stat_sum[:, 0:D], 1.0 / N, None, ALU.mult)
                dve.drain()
                dve.tensor_tensor(sq_m, mean, mean, ALU.mult)
                dve.drain()
                dve.scalar_tensor_tensor(out=var, in0=stat_sum[:, D:2 * D], scalar=1.0 / N, in1=sq_m,
                                         op0=ALU.mult, op1=ALU.subtract).then_inc(bn_var, 1)
                dve.wait_ge(bn_std, 1)
                dve.wait_ge(vecs_in, 48)
                dve.reciprocal(rstd, bn[:, 4, :])
                dve.drain()
                dve.tensor_tensor(bn_ab[:, 0, :], rstd, vecs[:, 1, :], ALU.mult)
                dve.tensor_tensor(bn[:, 5, :], mean, vecs[:, 0, :], ALU.add)
                dve.drain()
                dve.tensor_tensor(bn[:, 6, :], vecs[:, 0, :], bn[:, 5, :], ALU.subtract)
                dve.drain()
                dve.tensor_tensor(bn[:, 7, :], bn[:, 6, :], bn_ab[:, 0, :], ALU.mult)
                dve.drain()
                dve.tensor_tensor(bn_ab[:, 1, :], bn[:, 7, :], vecs[:, 2, :], ALU.add).then_inc(bn_row, 1)
                dve.wait_ge(bn_psum, 1)
                dve.tensor_copy(bn_b[:, :], ps_c[:, 0:D])
                dve.tensor_copy(t3(b_rows[:, :], D), over_r(bn_ab[:, 1, :], 512 // D))
                dve.wait_ge(cnt_std, 1)
                dve.reciprocal(dis_dst[:, :], dis_dst[:, :])
                dve.drain().then_inc(vecs_copied, 1)
                dve.tensor_scalar(rec[:, :, CNT], dis_dst[:, :], -1.0, None, ALU.add)
                for j in range(BLOCKS - 1, -1, -1):
                    part = rec[:, j * TILES:(j + 1) * TILES, 0:D]
                    dve.tensor_tensor(part, part, over_r(bn_b[:, :], TILES), ALU.mult).then_inc(o_scaled, 1)
                dve.drain()

                def scale_shift(chunk):
                    m, s, _, s3, u3 = chunk
                    v, y, t = nw[s][:, 3, :], nw[s][:, 4, :], nw[s][:, 6, :]
                    dve.wait_ge(q["landed"][s3], (u3 + 1) * 32)
                    row_stats(dve, xd[s3], D, s)
                    dve.drain()
                    dve.tensor_scalar(v, nw[s][:, 2, :], 1.0 / D, LN_EPS, ALU.mult, ALU.add)
                    dve.drain()
                    dve.tensor_scalar(t.bitcast(I32), v.bitcast(I32), 1, None, ALU.arith_shift_right)
                    dve.drain()
                    dve.tensor_scalar(y.bitcast(I32), t.bitcast(I32), -1.0, RSQRT_MAGIC, ALU.mult, ALU.add)
                    dve.drain()
                    for _ in range(3):
                        dve.scalar_tensor_tensor(out=t, in0=y, scalar=-0.5, in1=y, op0=ALU.mult, op1=ALU.mult)
                        dve.drain()
                        dve.tensor_tensor(t, t, v, ALU.mult)
                        dve.drain()
                        dve.scalar_tensor_tensor(out=y, in0=t, scalar=1.5, in1=y, op0=ALU.add, op1=ALU.mult)
                        dve.drain()
                    dve.scalar_tensor_tensor(out=nw[s][:, 5, :], in0=nw[s][:, 0, :], scalar=-0.5,
                                             in1=y, op0=ALU.mult, op1=ALU.mult).then_inc(x1_scale, 1)

                def add_h(chunk):
                    m, s, _, s3, _ = chunk
                    dve.wait_ge(x1_h, m + 1)
                    dve.tensor_tensor(t3(hd[s], D), t3(hd[s], D), rows_of(ad[s3]), ALU.add).then_inc(x1_z, 1)

                def add_x(chunk):
                    m, s, u, s3, _ = chunk
                    if not first_use(u):
                        dve.wait_ge(q["stored"][s], u * 16)
                    dve.tensor_scalar(t3(od[s], ROW)[:, :, D], t3(ad[s3], ROW)[:, :, CNT], 1.0, None, ALU.add)
                    dve.wait_ge(x1_gelu, m + 2)
                    dve.tensor_tensor(rows_of(od[s]), t3(xd[s3][:, 0:ROWS * D], D), t3(hd[s], D), ALU.add)
                    dve.drain().then_inc(q["made"][s], 1)
                    dve.drain().then_inc(q["free"][s3], 1)

                def step(at):
                    if at(2):
                        add_x(at(2))
                    if at(0):
                        scale_shift(at(0))
                    if at(1):
                        add_h(at(1))
                for s in range(3):
                    dve.sem_inc(q["free"][s], 1)
                over_chunks(dve, step)

        idx2_staged = sem("idx2_staged")
        gathered2 = [sem(f"gathered2_{s}") for s in range(GROUPS)]
        x1g_free = [sem(f"x1g_free{s}") for s in range(GROUPS)]
        var2_ready = sem("var2_ready")
        std2_ready = sem("std2_ready")
        scale2_ready = sem("scale2_ready")
        h2_ready = sem("h2_ready")
        rows2 = sem("rows2")
        rows2_t = sem("rows2_t")
        run2 = sem("run2")
        carry2 = sem("carry2")
        with nc.Block() as block:
            @block.gpsimd
            def _(pool):
                with pool.Fori(0, BLOCKS) as k:
                    for g in range(GROUPS):
                        s = g
                        wait_alone(pool, idx2_staged, k * GROUPS + (g + 1))
                        wait_alone(pool, x1g_free[g], k + 1)
                        for t in range(GROUP):
                            pool.indirect_dma_start(
                                xg[s][:, t * ROW:(t + 1) * ROW], None, x1t,
                                bass.IndirectOffsetOnAxis(ap=idx_stage[s][:, t:t + 1].bitcast(U32), axis=0),
                                bounds_check=N - 1, oob_is_err=False).then_inc(gathered2[s], 16)

            @block.scalar
            def _(act):
                with act.Fori(0, BLOCKS) as k:
                    for g in range(GROUPS):
                        s, n = g, k * GROUPS + (g + 1)
                        act.wait_ge(var2_ready, n)
                        act.activation(small[:, 3, 0:GROUP], small[:, 2, 0:GROUP], ACT.Sqrt, bias=eps[:, :],
                                       scale=1.0 / D).then_inc(std2_ready, 1)
                        wait_alone(act, scale2_ready, n)
                        for r in range(GROUP):
                            last = act.activation(rec[:, bass.ds(k * TILES + (g * GROUP + r), 1), 0:D]
                                                  .rearrange("p t c -> p (t c)"), xg[s][:, r * ROW:r * ROW + D], ACT.Relu,
                                                  bias=small[:, 5, r:r + 1], scale=small[:, 4, r:r + 1])
                        last.then_inc(h2_ready, 1)
                        act.drain().then_inc(x1g_free[s], 1)

            @block.tensor
            def _(pe):
                with pe.Fori(0, BLOCKS) as k:
                    wait_alone(pe, rows2, k + 1)
                    for j in range(2):
                        last = pe.transpose(ps_c[0:D, j * P:(j + 1) * P], pk[:, j, 0:D], ident[:, :])
                    last.then_inc(rows2_t, 1)
                    wait_alone(pe, run2, k + 1)
                    pe.transpose(ps_e[:, 0:D], run_v[0:D, 0:P], ident[0:D, 0:D]).then_inc(carry2, 1)

            @block.vector
            def _(dve):
                dve.memset(run_v[:, :], 0.0)
                for g in range(GROUPS):
                    dve.sem_inc(x1g_free[g], 1)
                    dve.tensor_copy(idx_stage[g][:, 0:GROUP], src_i[:, g * GROUP:(g + 1) * GROUP]).then_inc(idx2_staged, 1)
                with dve.Fori(0, BLOCKS) as k:
                    blk = bass.ds(k * TILES, TILES)
                    for g in range(GROUPS):
                        s, n = g, k * GROUPS + (g + 1)
                        dve.wait_ge(gathered2[g], (k + 1) * (GROUP * 16))
                        dve.tensor_copy(idx_stage[g][:, 0:GROUP], src_i[:, bass.ds((k + 1) * TILES + g * GROUP, GROUP)])\
                            .then_inc(idx2_staged, 1)
                        for r in range(GROUP):
                            dve.bn_stats(stats[:, r, :], xg[s][:, r * ROW:r * ROW + D])
                        dve.drain()
                        norm_sums(dve, stats, small, GROUP).then_inc(var2_ready, 1)
                        dve.wait_ge(std2_ready, n)
                        rstd, scale, shift = small[:, 6, 0:GROUP], small[:, 4, 0:GROUP], small[:, 5, 0:GROUP]
                        dve.reciprocal(rstd, small[:, 3, 0:GROUP])
                        dve.drain()
                        dve.tensor_tensor(scale, rstd, t3(xg[s][:, 0:GROUP * ROW], ROW)[:, :, D], ALU.mult)
                        dve.drain()
                        dve.scalar_tensor_tensor(out=shift, in0=small[:, 0, 0:GROUP], scalar=-0.5, in1=scale,
                                                 op0=ALU.mult, op1=ALU.mult).then_inc(scale2_ready, 1)
                    dve.wait_ge(h2_ready, (k + 1) * GROUPS)
                    for c in range(D):
                        col = rec[:, blk, c]
                        dve.tensor_tensor_scan(col, same[:, blk], col, 0.0, ALU.mult, ALU.add)
                    dve.drain()
                    at_end = bass.ds(k * TILES + TILES - 1, 1)
                    dve.tensor_copy(pk[:, 0, 0:D], rec[:, at_end, 0:D].rearrange("p t c -> p (t c)"))
                    dve.tensor_copy(pk[:, 1, 0:D], first[:, at_end].to_broadcast([P, D]))
                    dve.drain().then_inc(rows2, 1)
                    dve.wait_ge(rows2_t, k + 1)
                    scan_over_partitions(dve, row_v, run_v, D, ALU.mult, ALU.add, ps_c).then_inc(run2, 1)
                    dve.wait_ge(carry2, k + 1)
                    dve.tensor_copy(carry[:, 0:D], ps_e[:, 0:D])
                    dve.drain()
                    w3 = t3(wide, D)
                    dve.tensor_tensor(w3, over_c(first[:, blk], D), over_r(carry[:, 0:D], TILES), ALU.mult)
                    dve.drain()
                    dve.tensor_tensor(w3, w3, rec[:, blk, 0:D], ALU.add)
                    dve.drain()
                    dve.tensor_tensor(rec[:, blk, 0:D], w3, over_c(dis_dst[:, blk], D), ALU.mult)
                    dve.drain()

        m_stored = [sem(f"m_stored{j}") for j in range(2)]
        m_blocks = sem("m_blocks")
        out_var = sem("out_var")
        out_std = sem("out_std")
        out_scale = sem("out_scale")
        out_h = sem("out_h")
        out_s = sem("out_s")
        s_psum = sem("s_psum")
        sT_ready = sem("sT_ready")
        y_psum = sem("y_psum")
        y_taken = sem("y_taken")
        f = dense_sems("out")
        with nc.Block() as block:
            @block.gpsimd
            def _(pool):
                scatter_blocks(pool, m_stored, m_blocks)

            @block.sync
            def _(sp):
                dense_loads(sp, f, x1t, ROW, xd, m_blocks)

            @block.scalar
            def _(act):
                def step(at):
                    if at(0):
                        m, s, u, s3, _ = at(0)
                        act.wait_ge(out_var, m + 1)
                        act.activation(nw[s][:, 3, 0:ROWS], nw[s][:, 2, 0:ROWS], ACT.Sqrt, bias=eps[:, :],
                                       scale=1.0 / D).then_inc(out_std, 1)
                        act.wait_ge(out_scale, m + 1)
                        if not first_use(u):
                            act.wait_ge(s_psum, m - 1)
                        normalize_rows(act, xd[s3], ROW, s, range(ROWS)).then_inc(out_h, 1)
                    if at(1):
                        m = at(1)[0]
                        act.wait_ge(s_psum, m + 1)
                        act.activation(sT, ps_t[:, :], ACT.Copy).then_inc(sT_ready, 1)
                    if at(2):
                        dense_store(act, f, out, D, at(2))
                over_chunks(act, step)
                for s in range(2):
                    act.wait_ge(f["stored"][s], 16 * ((CHUNKS + 1 - s) // 2))

            @block.tensor
            def _(pe):
                def step(at):
                    if at(0):
                        m, s, _, _, _ = at(0)
                        wait_alone(pe, out_s, m + 1)
                        for j in range(ROWS // 2):
                            last = pe.transpose(ps_t[:, j * P:(j + 1) * P], hd[s][:, j * P:(j + 1) * P], ident[:, :])
                        last.then_inc(s_psum, 1)
                        pe.wait_ge(y_taken, m + 1)
                        pe.wait_ge(sT_ready, m + 1)
                        for j in range(ROWS // 2):
                            last = pe.matmul(ps_z[:, j * P:(j + 1) * P], sT[:, j * P:(j + 1) * P], w_2[:, :],
                                             start=True, stop=True)
                        last.then_inc(y_psum, 1)
                over_chunks(pe, step)

            @block.vector
            def _(dve):
                def scale_shift(chunk):
                    m, s, _, s3, u3 = chunk
                    dis, rstd, inv_deg = t3(xd[s3], ROW)[:, :, D], nw[s][:, 6, 0:ROWS], nw[s][:, 7, 0:ROWS]
                    scale, shift = nw[s][:, 4, 0:ROWS], nw[s][:, 5, 0:ROWS]
                    dve.wait_ge(f["landed"][s3], (u3 + 1) * 32)
                    row_stats(dve, xd[s3], ROW, s).then_inc(out_var, 1)
                    dve.tensor_tensor(inv_deg, dis, dis, ALU.mult)
                    dve.wait_ge(out_std, m + 1)
                    dve.reciprocal(rstd, nw[s][:, 3, 0:ROWS])
                    dve.drain()
                    dve.tensor_tensor(scale, rstd, inv_deg, ALU.mult)
                    dve.drain()
                    dve.scalar_tensor_tensor(out=shift, in0=nw[s][:, 0, 0:ROWS], scalar=-0.5, in1=scale,
                                             op0=ALU.mult, op1=ALU.mult).then_inc(out_scale, 1)

                def add_sum(chunk):
                    m, s, _, s3, _ = chunk
                    dve.wait_ge(out_h, m + 1)
                    dve.tensor_tensor(t3(hd[s], D), t3(hd[s], D), rows_of(ad[s3]), ALU.add).then_inc(out_s, 1)

                def add_bias(chunk):
                    m, s, u, s3, _ = chunk
                    if not first_use(u):
                        dve.wait_ge(f["stored"][s], u * 16)
                    dve.tensor_tensor(t3(od[s][:, 0:ROWS * D], D), rows_of(xd[s3]), over_r(b2_b[:, :], ROWS), ALU.add)
                    dve.drain().then_inc(f["free"][s3], 1)

                def finish(chunk):
                    m, s, _, _, _ = chunk
                    dve.wait_ge(y_psum, m + 1)
                    dve.tensor_tensor(od[s][:, 0:ROWS * D], od[s][:, 0:ROWS * D], ps_z[:, :], ALU.add)\
                        .then_inc(f["made"][s], 1)
                    dve.drain().then_inc(y_taken, 1)

                def step(at):
                    if at(0):
                        scale_shift(at(0))
                    if at(2):
                        finish(at(2))
                    if at(1):
                        add_sum(at(1))
                        add_bias(at(1))
                for s in range(3):
                    dve.sem_inc(f["free"][s], 1)
                dve.sem_inc(y_taken, 1)
                over_chunks(dve, step)


_INS = ["x", "src", "dst", "edge_attr_16", "L0_gnn_W_l", "L0_gnn_b_l", "L0_gnn_W_r", "L0_gnn_b_r", "L0_gnn_W_e",
        "L0_gnn_att", "L0_gnn_bias", "L0_gnn_gamma", "L0_gnn_beta", "L1_gnn_W", "L1_gnn_b"]


def kernel(**inputs):
    import numpy as np
    import concourse.bacc as bacc
    from concourse.bass_utils import run_bass_kernel_spmd

    arrays = {name: np.ascontiguousarray(inputs[name]) for name in _INS}
    pad = EP - E
    arrays["src"] = np.concatenate([arrays["src"], np.zeros(pad, np.int32)])
    arrays["dst"] = np.concatenate([np.full(1, -1, np.int32), arrays["dst"], np.full(pad + 1, N, np.int32)])
    arrays["edge_attr_16"] = np.concatenate([arrays["edge_attr_16"], np.zeros((pad, ED), np.float32)])

    nc = bacc.Bacc("TRN2", target_bir_lowering=False, num_devices=1)
    aps = [nc.dram_tensor(f"in_{n}", arrays[n].shape, mybir.dt.from_np(arrays[n].dtype), kind="ExternalInput").ap()
           for n in _INS]
    agg = nc.dram_tensor("agg", (NT, ROW), F32, kind="Internal").ap()
    x1t = nc.dram_tensor("x1t", (N, ROW), F32, kind="Internal").ap()
    out = nc.dram_tensor("out_x", (N, D), F32, kind="ExternalOutput").ap()
    build(nc, *aps, agg, x1t, out)
    r = run_bass_kernel_spmd(nc, [{f"in_{n}": arrays[n] for n in _INS}], core_ids=[0])
    return r.results[0]["out_x"]
```

```python
from contextlib import ExitStack

import concourse.bass as bass
from concourse import mybir

F32 = mybir.dt.float32
I32 = mybir.dt.int32
U32 = mybir.dt.uint32
ALU = mybir.AluOpType
ACT = mybir.ActivationFunctionType
AX_X = mybir.AxisListType.X

P = 128
N = 100000
E = 50000
D = 64
ED = 16
H = 4
C = D // H
TILES = 49
BLOCKS = -(-E // (P * TILES))
EP = BLOCKS * P * TILES
GROUP = 7
GROUPS = TILES // GROUP
ALLT = BLOCKS * TILES
CNT = D
DEN = D + 1
REC = D + 1 + H
ROW = D + 1
ROWS = 24
DVE_ROWS = 4
DVE_ROWS_X = 7
CHUNK = P * ROWS
CHUNKS = -(-N // CHUNK)
HALF = ROWS // 2
PIECES = 2 * (CHUNKS - 1) // BLOCKS
assert PIECES * BLOCKS == 2 * (CHUNKS - 1) and PIECES == GROUPS + 1
PIECES_X1 = 2
EARLY = 1 + BLOCKS * PIECES_X1 // 2
STAT_STEP = -(-2 * TILES // (GROUPS - 1))
ZROWS = -(-N // (P * (BLOCKS - 1) * GROUPS))
NT = P * ZROWS * (BLOCKS - 1) * GROUPS
BIG = 1.0e30
SKIP = float(1 << 20)
LN_EPS = 1e-5
BN_EPS = 1e-5
SLOPE = 0.2


def build(nc, x, src, dst, ea, W_l, b_l, W_r, b_r, W_e, att, bias, gamma, beta, W2, b2, agg, x1t, out):
    ctx = ExitStack()
    with ctx:
        def sb(name, shape, dt=F32):
            return ctx.enter_context(nc.sbuf_tensor(name, shape, dt))

        def psum(name, shape):
            return ctx.enter_context(nc.psum_tensor(name, shape, F32))

        def sem(name):
            return ctx.enter_context(nc.semaphore(name))

        waits_passed = sem("waits_passed")

        def wait_alone(eng, signal, count):
            eng.wait_ge(signal, count)
            eng.sem_inc(waits_passed, 1)

        rec_flat = sb("rec", [P, ALLT * REC])
        rec = rec_flat[:, :].rearrange("p (t c) -> p t c", c=REC)
        src_i = sb("src_i", [P, ALLT + TILES], I32)
        row_i = sb("row_i", [P, ALLT], I32)
        dstg_i = sb("dstg_i", [P, ALLT + TILES], I32)
        same = sb("same", [P, ALLT])
        first = sb("first", [P, ALLT])
        pen = sb("pen", [P, 2, TILES])
        is_end = sb("is_end", [P, ALLT])
        dis_dst = sb("dis_dst", [P, ALLT])
        idx_stage = [sb(f"idx_stage{s}", [P, 2 * GROUP], I32) for s in range(GROUPS)]
        ident = sb("ident", [P, P])
        ones = sb("ones", [1, P])
        eps = sb("eps", [P, 1])
        w_h = sb("w_h", [P, 2 * D])
        w_ea = sb("w_ea", [GROUP * ED + 2, GROUP * 2 * D])
        w_2 = sb("w_2", [P, 2 * D])
        block_first = sb("block_first", [1, BLOCKS], I32)
        chunk_first = sb("chunk_first", [1, CHUNKS], I32)
        blocks_f = sb("blocks_f", [1, CHUNKS])
        blocks_needed = sb("blocks_needed", [1, CHUNKS], I32)
        att_b = sb("att_b", [P, D])
        b2_b = sb("b2_b", [P, D])
        bn_b = sb("bn_b", [P, D])
        b_rows = w_ea[0:1, 0:512]
        norm_x = sb("norm_x", [P, 2, CHUNKS * ROWS])
        stat_sum = sb("stat_sum", [1, 2 * D])
        ea_in = [sb(f"ea_in{s}", [P, GROUP * ED + 2]) for s in range(2)]
        ea_t = sb("ea_t", [GROUP * ED + 2, P])
        stats = sb("stats", [P, 2 * GROUP, 6])
        small = [sb(f"small{j}", [P, 7, 2 * GROUP]) for j in range(3)]
        small = [small[g % 2] for g in range(GROUPS - 1)] + [small[2]]
        pk = sb("pk", [P, 2, REC])
        pm = sb("pm", [P, 2, H])
        row_m = sb("row_m", [H, 2 * P])
        run_m = sb("run_m", [H, P + 1])
        row_v = sb("row_v", [REC, 2 * P])
        run_v = sb("run_v", [REC, P + 1])
        carry = sb("carry", [P, REC])
        statd = sb("statd", [P, ROWS, 6])
        nw = [sb(f"nw{s}", [P, 8, ROWS]) for s in range(2)]
        vecs = sb("vecs", [1, 3, D])
        work = sb("work", [P, 8 * ROWS * ROW + 3 * ROWS * D])

        def pieces(sizes, at=0):
            views = []
            for n in sizes:
                views.append(work[:, at:at + n])
                at += n
            return views

        dense = pieces([ROWS * ROW] * 8 + [ROWS * D] * 3)
        xd, ad, od, hd, sT = dense[0:4], dense[4:6], dense[6:8], dense[8:10], dense[10]
        bn, bn_ab = (sT[0:1, a * D:b * D].rearrange("p (j c) -> p j c", c=D) for a, b in ((0, 8), (8, 10)))
        edge_sizes = [2 * GROUP * D] * (GROUPS + 2) + [GROUP * P, GROUP * D, TILES * D] + [TILES * H] * 5 + \
            [3 * TILES * H, H * (TILES + 1), TILES]
        edge = pieces(edge_sizes)
        zero = work[:, sum(edge_sizes):sum(edge_sizes) + ZROWS * ROW]
        x_rows = work[:, sum(edge_sizes) + ZROWS * ROW:][:, 0:ROWS * ROW]
        dst_i, prev_i, next_i = (v.bitcast(I32) for v in pieces([ALLT] * 3))
        block_in = work[0:1, 3 * ALLT:3 * ALLT + CHUNKS * BLOCKS].rearrange("p (m k) -> p m k", k=BLOCKS)
        xg = edge[0:GROUPS]
        edge = edge[GROUPS - 3:]
        sq = edge[3].rearrange("p (t c) -> p t c", c=D)
        hn, hT = edge[4], edge[5]
        zs = edge[6].rearrange("p (t c) -> p t c", c=D)
        wide = edge[7]
        logit, rfac, ffac = (v.rearrange("p (h t) -> p h t", h=H) for v in edge[8:11])
        ffac_t, wide_d = (v.rearrange("p (t h) -> p t h", h=H) for v in edge[11:13])
        expo = edge[13].rearrange("p (j h t) -> p j h t", j=3, h=H)
        mx = edge[14].rearrange("p (h t) -> p h t", h=H)
        end_blk = edge[15]

        ps_t = psum("ps_t", [P, 1536])
        ps_z = psum("ps_z", [P, 1536])
        ps_e = psum("ps_e", [P, 512])
        ps_c = psum("ps_c", [P, 512])
        ps_o = [ps_t[0:1, 1024:1024 + D], ps_z[0:1, 1024:1024 + D]]

        def t3(ap, c):
            return ap.rearrange("p (t c) -> p t c", c=c)

        def rows_of(ap):
            return t3(ap, ROW)[:, :, 0:D]

        def over_c(ap, n):
            return ap.unsqueeze(len(ap.shape)).to_broadcast(list(ap.shape) + [n])

        def over_r(ap, n):
            return ap.unsqueeze(1).to_broadcast([ap.shape[0], n] + list(ap.shape[1:]))

        edges_in = sem("edges_in")
        weights_in = sem("weights_in")
        ident_zero = sem("ident_zero")
        chunks_known = sem("chunks_known")
        agg_zeroed = sem("agg_zeroed")
        WEIGHTS = 3 + GROUP + 3 * GROUP + 4
        with nc.Block() as block:
            @block.sync
            def _(sp):
                def per_edge(ap):
                    return ap.rearrange("(k p t) -> p k t", p=P, t=TILES)

                def tile3(t):
                    return t[:, 0:ALLT].rearrange("p (k t) -> p k t", t=TILES)
                sp.dma_start(tile3(dst_i), per_edge(dst[1:1 + EP])).then_inc(edges_in, 16)
                sp.dma_start(tile3(prev_i), per_edge(dst[0:EP])).then_inc(edges_in, 16)
                sp.dma_start(tile3(next_i), per_edge(dst[2:2 + EP])).then_inc(edges_in, 16)
                sp.dma_start(tile3(src_i), per_edge(src)).then_inc(edges_in, 16)
                every = dst[1:1 + EP].rearrange("(k r) -> k r", r=P * TILES)
                sp.dma_start(block_first[:, :], every[:, 0:1].rearrange("k o -> o k"),
                             allow_slow_non_contiguous=True).then_inc(edges_in, 16)

            @block.gpsimd
            def _(pool):
                pool.memset(ident[:, :], 0.0).then_inc(ident_zero, 1)
                pool.wait_ge(ident_zero, 1)
                pool.affine_select(out=ident[:, :], in_=ident[:, :], compare_op=ALU.not_equal, fill=1.0,
                                   base=0, pattern=[[-1, P]], channel_multiplier=1).then_inc(ident_zero, 1)
                pool.iota(chunk_first[:, :], pattern=[[-CHUNK, CHUNKS]], base=(CHUNKS - 1) * CHUNK,
                          channel_multiplier=0).then_inc(chunks_known, 1)
                pool.wait_ge(chunks_known, 1)
                pool.memset(chunk_first[:, 0:1], N - CHUNK).then_inc(chunks_known, 1)
                pool.wait_ge(ident_zero, 2)

            @block.vector
            def _(dve):
                dve.memset(zero, 0.0)
                dve.memset(w_h[:, :], 0.0)
                dve.memset(w_ea[:, :], 0.0)
                dve.memset(w_2[:, :], 0.0)
                dve.memset(ones[:, :], 1.0)
                dve.memset(eps[:, :], LN_EPS)
                dve.memset(stat_sum[:, :], 0.0)
                dve.memset(run_m[:, :], -BIG)
                dve.memset(run_v[:, :], 0.0)
                for s in range(2):
                    dve.memset(ea_in[s][:, GROUP * ED:GROUP * ED + 2], 1.0)
                dve.memset(src_i[:, ALLT:ALLT + TILES], 0)
                dve.memset(dstg_i[:, ALLT:ALLT + TILES], 0)
                dve.wait_ge(edges_in, 80)
                dve.wait_ge(chunks_known, 2)
                dve.tensor_tensor(same[:, :], dst_i[:, :], prev_i[:, :], ALU.is_equal)
                dve.tensor_tensor(is_end[:, :], dst_i[:, :], next_i[:, :], ALU.not_equal)
                dve.tensor_tensor(block_in, over_r(block_first[:, :], CHUNKS),
                                  over_c(chunk_first[:, :], BLOCKS), ALU.is_ge)
                before = t3(prev_i[:, :], TILES)[:, :, 0]
                dve.tensor_tensor(t3(first[:, :], TILES), t3(dst_i[:, :], TILES), over_c(before, TILES), ALU.is_equal)
                dve.tensor_scalar(dstg_i[:, 0:ALLT], dst_i[:, :], float(N - 1), None, ALU.min)
                dve.drain()
                dve.reduce_sum(blocks_f[:, :], block_in, AX_X)
                dve.tensor_scalar(dis_dst[:, :], is_end[:, :], -SKIP, SKIP, ALU.mult, ALU.add)
                dve.drain()
                dve.tensor_copy(blocks_needed[:, :], blocks_f[:, :])
                dve.tensor_tensor(row_i[:, :], dst_i[:, :], dis_dst[:, :], ALU.add)
                dve.drain()

        def chunk_at(ap, w, m):
            start = N - CHUNK if isinstance(m, int) and m == 0 else (CHUNKS - 1 - m) * CHUNK if isinstance(m, int) \
                else (CHUNKS - 1) * CHUNK - m * CHUNK
            return ap[bass.ds(start, CHUNK), :].rearrange("(p r) c -> p (r c)", p=P)

        def load_half(sp, table, w, chunk, h, n, landed, taken):
            half = slice(h * HALF * w, (h + 1) * HALF * w)
            if n is not None:
                wait_alone(sp, taken, n - 1)
            sp.dma_start(x_rows[:, half], chunk_at(table, w, chunk)[:, half]).then_inc(landed[h], 16)

        def load_halves(sp, k, i, pieces, table, w, landed, taken):
            load_half(sp, table, w, k * (pieces // 2) + (1 + i // 2), i % 2, k * pieces + (2 + i), landed, taken)

        def half_sums(dve, chunk, h, w, landed, taken):
            wait_alone(dve, landed[h], (chunk + 1) * 16)
            for r in range(h * HALF, (h + 1) * HALF):
                dve.bn_stats(statd[:, r, :], x_rows[:, r * w:r * w + D])
            dve.drain().then_inc(taken, 1)
            if h:
                at = bass.ds(chunk * ROWS, ROWS)
                norm_sums(dve, statd, nw[0], ROWS, norm_x[:, 1, at], norm_x[:, 0, at])

        def slot_use(k, g):
            return k * (GROUPS - GROUPS // 2) + g // 2 if g % 2 == 0 else k * (GROUPS // 2) + g // 2

        def norm_sums(dve, st, out, n, mean2=None, var_d=None):
            half = D // 2
            mean2 = out[:, 0, 0:n] if mean2 is None else mean2
            var_d = out[:, 2, 0:n] if var_d is None else var_d
            dve.tensor_tensor(mean2, st[:, 0:n, 1], st[:, 0:n, 4], ALU.add)
            dve.tensor_tensor(out[:, 1, 0:n], st[:, 0:n, 1], st[:, 0:n, 4], ALU.subtract)
            dve.tensor_tensor(out[:, 6, 0:n], st[:, 0:n, 2], st[:, 0:n, 5], ALU.add)
            dve.drain()
            dve.tensor_tensor(out[:, 1, 0:n], out[:, 1, 0:n], out[:, 1, 0:n], ALU.mult)
            dve.drain()
            return dve.scalar_tensor_tensor(out=var_d, in0=out[:, 1, 0:n], scalar=half / 2.0,
                                            in1=out[:, 6, 0:n], op0=ALU.mult, op1=ALU.add)

        def scan_over_partitions(dve, row, run, n, op0, op1, ps):
            dve.tensor_copy(row[0:n, :], ps[0:n, 0:2 * P])
            dve.tensor_copy(run[0:n, 0:1], run[0:n, P:P + 1])
            dve.drain()
            return dve.tensor_tensor_scan(run[0:n, 1:P + 1], row[0:n, P:2 * P], row[0:n, 0:P], run[0:n, 0:1], op0, op1)

        idx_staged = sem("idx_staged")
        gathered = [sem(f"gathered{s}") for s in range(GROUPS)]
        xg_free = [sem(f"xg_free{s}") for s in range(GROUPS)]
        ea_landed = [sem(f"ea_landed{s}") for s in range(2)]
        ea_turned = [sem(f"ea_turned{s}") for s in range(2)]
        var_ready = sem("var_ready")
        std_ready = sem("std_ready")
        scale_ready = sem("scale_ready")
        h_ready = sem("h_ready")
        hT_psum = sem("hT_psum")
        hT_ready = sem("hT_ready")
        ea_t_ready = sem("ea_t_ready")
        z_psum = sem("z_psum")
        z_ready = sem("z_ready")
        zs_free = sem("zs_free")
        max_rows = sem("max_rows")
        max_rows_t = sem("max_rows_t")
        max_run = sem("max_run")
        max_carry = sem("max_carry")
        expo_in = sem("expo_in")
        expo_out = sem("expo_out")
        sum_rows = sem("sum_rows")
        sum_rows_t = sem("sum_rows_t")
        sum_run = sem("sum_run")
        sum_carry = sem("sum_carry")
        o_ready = sem("o_ready")
        o_squared = sem("o_squared")
        degree_ready = sem("degree_ready")
        degree_std = sem("degree_std")
        o_blocks_made = sem("o_blocks_made")
        edges_done = sem("edges_done")
        x_landed = [sem(f"x_landed{h}") for h in range(2)]
        x_taken = sem("x_taken")
        carry_taken = sem("carry_taken")
        stats_psum = sem("stats_psum")

        def over_groups(eng, group, finish_block, before, peeled=0):
            def one_block(k, last):
                for g in range(1, GROUPS):
                    group(k, g)
                before(k, last)
                if not last:
                    group(k + 1, 0)
                finish_block(k)
            group(0, 0)
            for k in range(peeled):
                one_block(k, False)
            with eng.Fori(0, BLOCKS - 1 - peeled) as k:
                one_block(k + peeled if peeled else k, False)
            one_block(BLOCKS - 1, True)

        def over_chunks(eng, step, behind=2, late_from=None):
            peeled = 5

            def fixed(m):
                def at(lag):
                    c = m - lag
                    return (c, c % 2, c // 2, c % 4, c // 4) if 0 <= c < CHUNKS else None
                return at

            def looped(i, j):
                def at(lag):
                    c = j - lag
                    return (i * 4 + c, c % 2, i * 2 + c // 2, c % 4, i + c // 4)
                return at
            def take(at, m):
                if late_from is None:
                    step(at)
                else:
                    step(at, m >= late_from)
            for m in range(peeled):
                take(fixed(m), m)
            split = peeled if late_from is None else late_from
            for begin, end in ((peeled, split), (split, CHUNKS)):
                assert (end - begin) % 4 == 0
                if end > begin:
                    with eng.Fori((begin - peeled) // 4, (end - peeled) // 4) as i:
                        for j in range(peeled, peeled + 4):
                            take(looped(i, j), begin)
            for m in range(CHUNKS, CHUNKS + behind):
                take(fixed(m), m)

        def first_use(u):
            return isinstance(u, int) and u == 0

        def dense_sems(tag):
            return {n: [sem(f"{tag}_{n}{s}") for s in range(slots)]
                    for n, slots in (("landed", 4), ("free", 4), ("sums_landed", 2), ("sums_free", 2),
                                     ("made", 2), ("stored", 2))}

        def dense_loads(sp, q, table, w, tiles, stored_blocks):
            def load(at):
                if at(0):
                    m, s, u, s4, u4 = at(0)
                    sp.wait_ge(q["free"][s4], u4 + 1)
                    sp.dma_start(tiles[s4][:, 0:ROWS * w], chunk_at(table, w, m)).then_inc(q["landed"][s4], 16)
                    sp.wait_ge(q["sums_free"][s], u + 1)
                    sp.wait_ge(stored_blocks, sp.value_load(blocks_needed[0:1, bass.ds(m, 1)], min_val=1, max_val=BLOCKS))
                    sp.dma_start(ad[s], chunk_at(agg, ROW, m)).then_inc(q["sums_landed"][s], 16)
            over_chunks(sp, load)

        def dense_store(eng, q, table, w, chunk):
            m, s, u, _, _ = chunk
            eng.wait_ge(q["made"][s], u + 1)
            eng.dma_start(chunk_at(table, w, m), od[s][:, 0:ROWS * w]).then_inc(q["stored"][s], 16)
            if first_use(u) and s == 0:
                eng.wait_ge(q["stored"][0], 16)

        def scatter_blocks(pool, stored, stored_blocks, block_ready):
            def finished(j):
                pool.wait_ge(stored[j % 2], 16 * TILES * (j // 2 + 1))
                pool.sem_inc(stored_blocks, 1)
            for j in range(BLOCKS):
                pool.wait_ge(block_ready, j + 1)
                for t in range(TILES):
                    a = j * TILES + t
                    pool.indirect_dma_start(
                        agg, bass.IndirectOffsetOnAxis(ap=row_i[:, a:a + 1].bitcast(U32), axis=0),
                        rec[:, a, 0:ROW], None, bounds_check=N - 1, oob_is_err=False).then_inc(stored[j % 2], 16)
                    if j and t == 2:
                        finished(j - 1)
            finished(BLOCKS - 1)

        def row_stats(dve, tile, w, s):
            for r in range(ROWS):
                dve.bn_stats(statd[:, r, :], tile[:, r * w:r * w + D])
            dve.drain()
            return norm_sums(dve, statd, nw[s], ROWS)

        def normalize_rows(act, tile, w, s, rows):
            for r in rows:
                last = act.activation(hd[s][:, r * D:(r + 1) * D], tile[:, r * w:r * w + D], ACT.Relu,
                                      bias=nw[s][:, 5, r:r + 1], scale=nw[s][:, 4, r:r + 1])
            return last

        def scale_rows(dve, tile, w, s, rows):
            for r in range(rows):
                dve.tensor_scalar(hd[s][:, r * D:(r + 1) * D], tile[:, r * w:r * w + D],
                                  nw[s][:, 4, r:r + 1], nw[s][:, 5, r:r + 1], ALU.mult, ALU.add)

        bn_var = sem("bn_var")
        bn_std = sem("bn_std")
        bn_row = sem("bn_row")
        bn_psum = sem("bn_psum")
        o_stored = [sem(f"o_stored{j}") for j in range(2)]
        o_blocks = sem("o_blocks")
        vecs_in = sem("vecs_in")
        vecs_copied = sem("vecs_copied")
        x1_sum = sem("x1_sum")
        x1_scale = sem("x1_scale")
        x1_h = sem("x1_h")
        x1_z = sem("x1_z")
        x1_std = sem("x1_std")
        x1_gelu = sem("x1_gelu")
        q = dense_sems("x1")
        z = [ps_t, ps_z]
        oa = sT
        with nc.Block() as block:
            @block.sync
            def _(sp):
                ea_r = ea.rearrange("(k p t) c -> k p (t c)", p=P, t=TILES)

                for h in range(2):
                    load_half(sp, x, D, 0, h, None, x_landed, x_taken)

                def loads(k, last):
                    for g in range(GROUPS):
                        s, use = g % 2, slot_use(k, g)
                        sp.wait_ge(ea_turned[s], use + 1)
                        sp.dma_start(ea_in[s][:, 0:GROUP * ED],
                                     ea_r[bass.ds(k, 1), :, g * GROUP * ED:(g + 1) * GROUP * ED]
                                     .rearrange("k p c -> p (k c)")).then_inc(ea_landed[s], 16)
                        if not last:
                            sp.dma_start(agg[bass.ds((k * GROUPS + g) * (P * ZROWS), P * ZROWS), :]
                                         .rearrange("(p r) c -> p (r c)", p=P), zero).then_inc(agg_zeroed, 16)
                        load_halves(sp, k, g, PIECES, x, D, x_landed, x_taken)
                    load_halves(sp, k, GROUPS, PIECES, x, D, x_landed, x_taken)
                with sp.Fori(0, BLOCKS - 1) as k:
                    loads(k, False)
                loads(BLOCKS - 1, True)

                for j, v in enumerate((bias, gamma, beta)):
                    sp.dma_start(vecs[:, j, :], v.unsqueeze(0)).then_inc(vecs_in, 16)
                sp.wait_ge(edges_done, 1)
                dense_loads(sp, q, x, D, xd, o_blocks)

            @block.gpsimd
            def _(pool):
                with pool.Fori(0, BLOCKS) as k:
                    for g in range(GROUPS):
                        s = g
                        wait_alone(pool, idx_staged, k * GROUPS + (g + 1))
                        wait_alone(pool, xg_free[g], k + 1)
                        for t in range(GROUP):
                            for side in range(2):
                                a = (2 * t + side) * D
                                i = side * GROUP + t
                                pool.indirect_dma_start(
                                    xg[s][:, a:a + D], None, x,
                                    bass.IndirectOffsetOnAxis(ap=idx_stage[s][:, i:i + 1].bitcast(U32), axis=0),
                                    bounds_check=N - 1, oob_is_err=False).then_inc(gathered[s], 16)

                pool.wait_ge(agg_zeroed, 16 * (BLOCKS - 1) * GROUPS)
                scatter_blocks(pool, o_stored, o_blocks, o_blocks_made)

            @block.scalar
            def _(act):
                act.dma_start(w_h[0:D, 0:D], W_l).then_inc(weights_in, 16)
                act.dma_start(w_h[0:D, D:2 * D], W_l).then_inc(weights_in, 16)
                act.dma_start(w_h[D:2 * D, D:2 * D], W_r).then_inc(weights_in, 16)
                for j in range(GROUP):
                    act.dma_start(w_ea[j * ED:(j + 1) * ED, j * 2 * D + D:(j + 1) * 2 * D], W_e).then_inc(weights_in, 16)
                k0 = GROUP * ED
                for j in range(GROUP):
                    act.dma_start(w_ea[k0:k0 + 1, j * 2 * D:j * 2 * D + D], b_l.unsqueeze(0)).then_inc(weights_in, 16)
                    act.dma_start(w_ea[k0:k0 + 1, j * 2 * D + D:(j + 1) * 2 * D], b_l.unsqueeze(0)).then_inc(weights_in, 16)
                    act.dma_start(w_ea[k0 + 1:k0 + 2, j * 2 * D + D:(j + 1) * 2 * D], b_r.unsqueeze(0)).then_inc(weights_in, 16)
                act.dma_start(w_2[0:D, 0:D], W2).then_inc(weights_in, 16)
                act.dma_start(w_2[D:2 * D, D:2 * D], W2).then_inc(weights_in, 16)
                act.dma_start(att_b[:, :], att.rearrange("h c -> (h c)").partition_broadcast(P)).then_inc(weights_in, 16)
                act.dma_start(b2_b[:, :], b2.partition_broadcast(P)).then_inc(weights_in, 16)

                def normalize(k, g):
                    s, n = g, k * GROUPS + (g + 1)
                    act.wait_ge(var_ready, n)
                    act.activation(small[g][:, 3, :], small[g][:, 2, :], ACT.Sqrt, bias=eps[:, :],
                                   scale=1.0 / D).then_inc(std_ready, 1)
                    act.wait_ge(scale_ready, n)
                    act.wait_ge(hT_psum, n)
                    for r in range(2 * GROUP):
                        last = act.activation(hn[:, r * D:(r + 1) * D], xg[s][:, r * D:(r + 1) * D], ACT.Relu,
                                              bias=small[g][:, 5, r:r + 1], scale=small[g][:, 4, r:r + 1])
                    last.then_inc(h_ready, 1)
                    act.drain().then_inc(xg_free[s], 1)

                def take_z(k, g):
                    n = k * GROUPS + (g + 1)
                    wait_alone(act, z_psum, n)
                    z = t3(ps_z[:, 0:GROUP * 2 * D], 2 * D)
                    act.activation(rec[:, bass.ds(k * TILES + g * GROUP, GROUP), 0:D], z[:, :, 0:D], ACT.Copy)
                    act.wait_ge(zs_free, n)
                    act.activation(zs, z[:, :, D:2 * D], ACT.Copy).then_inc(z_ready, 1)

                def take_turned(k, g):
                    s, use, n = g % 2, slot_use(k, g), k * GROUPS + (g + 1)
                    act.wait_ge(ea_turned[s], use + 2)
                    act.activation(ea_t[:, :], ps_e[0:GROUP * ED + 2, 0:P], ACT.Copy).then_inc(ea_t_ready, 1)
                    act.wait_ge(hT_psum, n + 1)
                    act.activation(hT, ps_t[:, 0:GROUP * P], ACT.Copy).then_inc(hT_ready, 1)

                def group(k, g):
                    normalize(k, g)
                    if g:
                        take_z(k, g - 1)
                    take_turned(k, g)

                def finish_block(k):
                    act.wait_ge(expo_in, k + 1)
                    act.activation(expo, expo, ACT.Exp).then_inc(expo_out, 1)
                    act.wait_ge(degree_ready, k + 1)
                    act.activation(pen[:, 0, :], pen[:, 1, :], ACT.Sqrt).then_inc(degree_std, 1)
                    wait_alone(act, o_ready, k + 1)
                    act.activation(t3(wide, D), rec[:, bass.ds(k * TILES, TILES), 0:D], ACT.Square).then_inc(o_squared, 1)

                over_groups(act, group, finish_block, lambda k, last: take_z(k, GROUPS - 1))

                act.wait_ge(bn_var, 1)
                act.activation(norm_x[:, 0, :], norm_x[:, 0, :], ACT.Sqrt, bias=eps[:, :], scale=1.0 / D).then_inc(x1_std, 1)
                act.activation(bn[:, 4, :], bn[:, 1, :], ACT.Sqrt, bias=eps[0:1, :], scale=1.0).then_inc(bn_std, 1)

                def step(at):
                    if at(3):
                        dense_store(act, q, x1t, ROW, at(3))
                    if at(2):
                        m, s, u, _, _ = at(2)
                        act.wait_ge(x1_sum, m + 1)
                        if not first_use(u):
                            act.wait_ge(q["stored"][s], u * 16)
                        act.activation(rows_of(od[s]), t3(z[s][:, :], D), ACT.Gelu).then_inc(x1_gelu, 1)
                    if at(0):
                        m, s, u, s4, u4 = at(0)
                        act.wait_ge(x1_scale, m + 1)
                        if not first_use(u):
                            act.wait_ge(x1_z, m - 1)
                        act.wait_ge(q["landed"][s4], (u4 + 1) * 16)
                        normalize_rows(act, xd[s4], D, s, range(DVE_ROWS_X, ROWS)).then_inc(x1_h, 1)
                over_chunks(act, step, 3)
                for s in range(2):
                    act.wait_ge(q["stored"][s], 16 * ((CHUNKS + 1 - s) // 2))

            @block.tensor
            def _(pe):
                for s in range(2):
                    pe.sem_inc(ea_turned[s], 1)
                pe.sem_inc(hT_psum, 1)
                pe.sem_inc(stats_psum, 1)
                pe.wait_ge(weights_in, WEIGHTS * 16)

                def group(k, g):
                    s, use, n = g % 2, slot_use(k, g), k * GROUPS + (g + 1)
                    if g == 1 and not (isinstance(k, int) and k == 0):
                        wait_alone(pe, carry_taken, k)
                    pe.wait_ge(ea_landed[s], (use + 1) * 16)
                    pe.transpose(ps_e[0:GROUP * ED + 2, 0:P], ea_in[s][:, :], ident[:, :]).then_inc(ea_turned[s], 1)
                    pe.wait_ge(h_ready, n)
                    for t in range(GROUP):
                        last = pe.transpose(ps_t[:, t * P:(t + 1) * P], hn[:, t * P:(t + 1) * P], ident[:, :])
                    last.then_inc(hT_psum, 1)
                    pe.wait_ge(ea_t_ready, n)
                    pe.wait_ge(z_ready, n)
                    for a, b in ((0, 4), (4, GROUP)):
                        pe.matmul(ps_z[:, a * P:b * P], ea_t[:, :], w_ea[:, a * P:b * P], start=True, stop=False,
                                  skip_group_check=True)
                    pe.wait_ge(hT_ready, n)
                    for t in range(GROUP):
                        last = pe.matmul(ps_z[:, t * P:(t + 1) * P], hT[:, t * P:(t + 1) * P], w_h[:, :],
                                         start=False, stop=True, skip_group_check=True)
                    last.then_inc(z_psum, 1)
                    if g and not (isinstance(k, int) and k == 0):
                        node_sums(k - 1, (g - 1) * STAT_STEP, min(g * STAT_STEP, 2 * TILES))

                def node_sums(k, a, b):
                    if a == 0:
                        pe.wait_ge(o_ready, k + 1)
                    for i in range(a, b):
                        j, t = divmod(i, TILES)
                        if i == TILES:
                            wait_alone(pe, o_squared, k + 1)
                        rhs = rec[:, bass.ds(k * TILES + t, 1), 0:D].rearrange("p t c -> p (t c)") if j == 0 else \
                            wide[:, t * D:(t + 1) * D]
                        last = pe.matmul(ps_o[j], end_blk[:, t:t + 1], rhs, start=(t == 0), stop=(t == TILES - 1))
                    if b == 2 * TILES:
                        last.then_inc(stats_psum, 1)

                def finish_block(k):
                    wait_alone(pe, max_rows, k + 1)
                    for j in range(2):
                        last = pe.transpose(ps_c[0:H, j * P:(j + 1) * P], pm[:, j, :], ident[:, :])
                    last.then_inc(max_rows_t, 1)
                    wait_alone(pe, max_run, k + 1)
                    pe.transpose(ps_e[:, 0:H], run_m[:, 0:P], ident[0:H, 0:H]).then_inc(max_carry, 1)
                    wait_alone(pe, sum_rows, k + 1)
                    for j in range(2):
                        last = pe.transpose(ps_c[0:REC, j * P:(j + 1) * P], pk[:, j, :], ident[:, :])
                    last.then_inc(sum_rows_t, 1)
                    wait_alone(pe, sum_run, k + 1)
                    pe.transpose(ps_e[:, 0:REC], run_v[:, 0:P], ident[0:REC, 0:REC]).then_inc(sum_carry, 1)

                over_groups(pe, group, finish_block, lambda k, last: None, peeled=1)
                node_sums(BLOCKS - 1, 0, 2 * TILES)

                pe.wait_ge(bn_row, 1)
                pe.matmul(ps_c[:, 0:2 * D], ones[:, :], bn_ab[:, :, :].rearrange("p j c -> p (j c)"),
                          start=True, stop=True).then_inc(bn_psum, 1)
                pe.wait_ge(vecs_copied, 1)

                def step(at):
                    if at(0):
                        m, s, u, _, _ = at(0)
                        if not first_use(u):
                            pe.wait_ge(x1_gelu, m - 1)
                        for j in range(ROWS * D // 512):
                            pe.matmul(z[s][:, j * 512:(j + 1) * 512], ones[:, :], b_rows, start=True, stop=False)
                        pe.wait_ge(x1_z, m + 1)
                        for j in range(ROWS * D // 512):
                            last = pe.matmul(z[s][:, j * 512:(j + 1) * 512], ident[:, :], oa[:, j * 512:(j + 1) * 512],
                                             start=False, stop=True)
                        last.then_inc(x1_sum, 1)
                over_chunks(pe, step)

            @block.vector
            def _(dve):
                def stage_indices(k, g):
                    a = k * TILES + g * GROUP
                    dve.tensor_copy(idx_stage[g][:, 0:GROUP], src_i[:, bass.ds(a, GROUP)])
                    dve.tensor_copy(idx_stage[g][:, GROUP:2 * GROUP], dstg_i[:, bass.ds(a, GROUP)]).then_inc(idx_staged, 1)

                def sums_beside(k, i):
                    half_sums(dve, k * (PIECES // 2) + (1 + i // 2), i % 2, D, x_landed, x_taken)

                def layer_norm(k, g, beside=None):
                    s, n = g, k * GROUPS + (g + 1)
                    dve.wait_ge(gathered[g], (k + 1) * (2 * GROUP * 16))
                    stage_indices(k + 1, g)
                    for r in range(2 * GROUP):
                        dve.bn_stats(stats[:, r, :], xg[s][:, r * D:(r + 1) * D])
                    dve.drain()
                    norm_sums(dve, stats, small[g], 2 * GROUP).then_inc(var_ready, 1)
                    if beside is not None:
                        sums_beside(*beside)
                    dve.wait_ge(std_ready, n)
                    dve.reciprocal(small[g][:, 4, :], small[g][:, 3, :])
                    dve.drain()
                    dve.scalar_tensor_tensor(out=small[g][:, 5, :], in0=small[g][:, 0, :], scalar=-0.5, in1=small[g][:, 4, :],
                                             op0=ALU.mult, op1=ALU.mult).then_inc(scale_ready, 1)

                def logits(k, g):
                    n = k * GROUPS + (g + 1)
                    dve.wait_ge(z_ready, n + 1)
                    dve.scalar_tensor_tensor(out=sq[:, 0:GROUP, :], in0=zs, scalar=SLOPE, in1=zs,
                                             op0=ALU.mult, op1=ALU.max)
                    dve.drain().then_inc(zs_free, 1)
                    dve.tensor_tensor(sq[:, GROUP:2 * GROUP, :], sq[:, 0:GROUP, :], over_r(att_b[:, :], GROUP), ALU.mult)
                    dve.drain()
                    dve.reduce_sum(logit[:, :, g * GROUP:(g + 1) * GROUP].rearrange("p h t -> p t h"),
                                   sq[:, GROUP:2 * GROUP, :].rearrange("p t (h c) -> p t h c", h=H), AX_X)
                    dve.drain()

                for g in range(GROUPS):
                    dve.sem_inc(xg_free[g], 1)
                    stage_indices(0, g)
                dve.sem_inc(zs_free, 1)
                dve.sem_inc(z_ready, 1)

                def add_stats(k):
                    dve.wait_ge(stats_psum, k + 1)
                    for j in range(2):
                        part = stat_sum[:, j * D:(j + 1) * D]
                        dve.tensor_tensor(part, part, ps_o[j], ALU.add)

                def group(k, g):
                    if g == 1:
                        layer_norm(k, 1, (k, 0))
                    if 0 < g < GROUPS - 1:
                        layer_norm(k, g + 1, (k, g))
                    if g:
                        logits(k, g - 1)

                def before_next(k, last):
                    if not last:
                        layer_norm(k + 1, 0)
                    sums_beside(k, GROUPS - 1)
                    logits(k, GROUPS - 1)

                def finish_block(k):
                    blk = bass.ds(k * TILES, TILES)
                    add_stats(k)
                    dve.tensor_scalar(pen[:, 0, :], same[:, blk], -1.0, BIG, ALU.add, ALU.mult)
                    dve.tensor_scalar(pen[:, 1, :], first[:, blk], -1.0, BIG, ALU.add, ALU.mult)
                    dve.drain()
                    for h in range(H):
                        dve.tensor_tensor_scan(mx[:, h, 1:TILES + 1], pen[:, 0, :], logit[:, h, :], -BIG,
                                               ALU.add, ALU.max)
                    dve.drain()
                    dve.tensor_copy(pm[:, 0, :], mx[:, :, TILES])
                    dve.tensor_copy(pm[:, 1, :], pen[:, 1, TILES - 1:TILES].to_broadcast([P, H]))\
                        .then_inc(max_rows, 1)
                    dve.wait_ge(max_rows_t, k + 1)
                    scan_over_partitions(dve, row_m, run_m, H, ALU.add, ALU.max, ps_c).then_inc(max_run, 1)
                    dve.wait_ge(max_carry, k + 1)
                    dve.tensor_copy(mx[:, :, 0], ps_e[:, 0:H])
                    dve.drain()
                    came = over_c(mx[:, :, 0], TILES)
                    dve.tensor_tensor(rfac[:, :, :], came, over_r(pen[:, 1, :], H), ALU.add)
                    dve.drain()
                    dve.tensor_tensor(mx[:, :, 1:TILES + 1], mx[:, :, 1:TILES + 1], rfac[:, :, :], ALU.max)
                    dve.drain()
                    now = mx[:, :, 1:TILES + 1]
                    dve.tensor_tensor(expo[:, 0, :, :], mx[:, :, 0:TILES], now, ALU.subtract)
                    dve.tensor_tensor(expo[:, 1, :, :], came, now, ALU.subtract)
                    dve.tensor_tensor(expo[:, 2, :, :], logit, now, ALU.subtract)
                    dve.drain()
                    dve.tensor_scalar(expo, expo, 0.0, None, ALU.min).then_inc(expo_in, 1)
                    sums_beside(k, GROUPS)
                    dve.wait_ge(expo_out, k + 1)
                    dve.tensor_tensor(rfac[:, :, :], expo[:, 0, :, :], over_r(same[:, blk], H), ALU.mult)
                    dve.tensor_tensor(ffac[:, :, :], expo[:, 1, :, :], over_r(first[:, blk], H), ALU.mult)
                    ex_t = expo[:, 2, :, :].rearrange("p h t -> p t h")
                    heads = rec[:, blk, 0:D].rearrange("p t (h c) -> p t h c", h=H)
                    dve.tensor_tensor(heads, heads, over_c(ex_t, C), ALU.mult)
                    dve.tensor_copy(rec[:, blk, DEN:DEN + H], ex_t)
                    dve.tensor_scalar(rec[:, blk, CNT], same[:, blk], 0.0, 1.0, ALU.mult, ALU.add)
                    dve.tensor_copy(end_blk[:, :], is_end[:, blk])
                    dve.drain()
                    for c in range(REC):
                        decay = same[:, blk] if c == CNT else rfac[:, c // C if c < D else c - DEN, :]
                        col = rec[:, blk, c]
                        dve.tensor_tensor_scan(col, decay, col, 0.0, ALU.mult, ALU.add)
                    dve.drain()
                    at_end = bass.ds(k * TILES + TILES - 1, 1)
                    dve.tensor_copy(pk[:, 0, :], rec[:, at_end, :].rearrange("p t c -> p (t c)"))
                    last = ffac[:, :, TILES - 1]
                    dve.tensor_copy(pk[:, 1, 0:D].rearrange("p (h c) -> p h c", h=H), over_c(last, C))
                    dve.tensor_copy(pk[:, 1, DEN:DEN + H], last)
                    dve.tensor_copy(pk[:, 1, CNT:CNT + 1], first[:, at_end])
                    dve.tensor_copy(ffac_t[:, :, :], ffac[:, :, :].rearrange("p h t -> p t h"))
                    dve.drain().then_inc(sum_rows, 1)
                    dve.wait_ge(sum_rows_t, k + 1)
                    scan_over_partitions(dve, row_v, run_v, REC, ALU.mult, ALU.add, ps_c).then_inc(sum_run, 1)
                    dve.wait_ge(sum_carry, k + 1)
                    dve.tensor_copy(carry[:, :], ps_e[:, 0:REC]).then_inc(carry_taken, 1)
                    dve.drain()
                    w4 = wide.rearrange("p (t h c) -> p t h c", h=H, c=C)
                    dve.tensor_tensor(w4, over_c(ffac_t[:, :, :], C),
                                      over_r(carry[:, 0:D].rearrange("p (h c) -> p h c", h=H), TILES), ALU.mult)
                    dve.tensor_tensor(wide_d[:, :, :], ffac_t[:, :, :], over_r(carry[:, DEN:DEN + H], TILES), ALU.mult)
                    dve.scalar_tensor_tensor(out=rec[:, blk, CNT], in0=first[:, blk], scalar=carry[:, CNT:CNT + 1],
                                             in1=rec[:, blk, CNT], op0=ALU.mult, op1=ALU.add)
                    dve.drain()
                    dve.tensor_scalar(pen[:, 1, :], rec[:, blk, CNT], 1.0, None, ALU.add).then_inc(degree_ready, 1)
                    dve.tensor_tensor(rec[:, blk, 0:D], rec[:, blk, 0:D], t3(wide, D), ALU.add)
                    dve.scalar_tensor_tensor(out=wide_d[:, :, :], in0=wide_d[:, :, :], scalar=1e-16,
                                             in1=rec[:, blk, DEN:DEN + H], op0=ALU.add, op1=ALU.add)
                    dve.drain()
                    dve.reciprocal(wide_d[:, :, :], wide_d[:, :, :])
                    dve.drain()
                    dve.tensor_tensor(heads, heads, over_c(wide_d[:, :, :], C), ALU.mult).then_inc(o_ready, 1)
                    dve.wait_ge(degree_std, k + 1)
                    dve.reciprocal(dis_dst[:, blk], pen[:, 0, :])
                    dve.drain()
                    dve.tensor_scalar(rec[:, blk, CNT], dis_dst[:, blk], -1.0, None, ALU.add)
                    dve.drain().then_inc(o_blocks_made, 1)

                for j in range(2):
                    dve.memset(ps_o[j], 0.0)
                dve.drain()
                for h in range(2):
                    half_sums(dve, 0, h, D, x_landed, x_taken)
                layer_norm(0, 0)
                dve.wait_ge(weights_in, WEIGHTS * 16)
                over_groups(dve, group, finish_block, before_next)
                add_stats(BLOCKS)
                dve.drain().then_inc(edges_done, 1)

                mean, var, sq_m, rstd = (bn[:, j, :] for j in range(4))
                dve.tensor_scalar(mean, stat_sum[:, 0:D], 1.0 / N, None, ALU.mult)
                dve.drain()
                dve.tensor_tensor(sq_m, mean, mean, ALU.mult)
                dve.drain()
                dve.scalar_tensor_tensor(out=var, in0=stat_sum[:, D:2 * D], scalar=1.0 / N, in1=sq_m,
                                         op0=ALU.mult, op1=ALU.subtract).then_inc(bn_var, 1)
                dve.wait_ge(bn_std, 1)
                dve.wait_ge(vecs_in, 48)
                dve.reciprocal(rstd, bn[:, 4, :])
                dve.drain()
                dve.tensor_tensor(bn_ab[:, 0, :], rstd, vecs[:, 1, :], ALU.mult)
                dve.tensor_tensor(bn[:, 5, :], mean, vecs[:, 0, :], ALU.add)
                dve.drain()
                dve.tensor_tensor(bn[:, 6, :], vecs[:, 0, :], bn[:, 5, :], ALU.subtract)
                dve.drain()
                dve.tensor_tensor(bn[:, 7, :], bn[:, 6, :], bn_ab[:, 0, :], ALU.mult)
                dve.drain()
                dve.tensor_tensor(bn_ab[:, 1, :], bn[:, 7, :], vecs[:, 2, :], ALU.add).then_inc(bn_row, 1)
                dve.wait_ge(bn_psum, 1)
                dve.tensor_copy(bn_b[:, :], ps_c[:, 0:D])
                dve.tensor_copy(t3(b_rows, D), over_r(bn_ab[:, 1, :], 512 // D))
                dve.drain().then_inc(vecs_copied, 1)
                dve.wait_ge(x1_std, 1)

                def scale_shift(chunk):
                    m, s, u, s4, u4 = chunk
                    scale, shift, at = nw[s][:, 4, 0:ROWS], nw[s][:, 5, 0:ROWS], bass.ds(m * ROWS, ROWS)
                    if not first_use(u):
                        dve.wait_ge(x1_h, m - 1)
                    dve.reciprocal(scale, norm_x[:, 0, at])
                    dve.drain()
                    dve.scalar_tensor_tensor(out=shift, in0=norm_x[:, 1, at], scalar=-0.5,
                                             in1=scale, op0=ALU.mult, op1=ALU.mult)
                    dve.drain().then_inc(x1_scale, 1)
                    dve.wait_ge(q["landed"][s4], (u4 + 1) * 16)
                    scale_rows(dve, xd[s4], D, s, DVE_ROWS_X)

                def add_h(chunk):
                    m, s, u, _, _ = chunk
                    dve.wait_ge(q["sums_landed"][s], (u + 1) * 16)
                    if not (isinstance(m, int) and m == 0):
                        dve.wait_ge(x1_sum, m)
                    dve.tensor_tensor(t3(oa, D), rows_of(ad[s]), over_r(bn_b[:, :], ROWS), ALU.mult)
                    dve.tensor_scalar(nw[s][:, 7, 0:ROWS], t3(ad[s], ROW)[:, :, CNT], 1.0, None, ALU.add)
                    dve.drain().then_inc(q["sums_free"][s], 1)
                    dve.wait_ge(x1_h, m + 1)
                    dve.scalar_tensor_tensor(out=oa, in0=hd[s], scalar=0.0, in1=oa, op0=ALU.max, op1=ALU.add)\
                        .then_inc(x1_z, 1)

                def add_x(chunk):
                    m, s, u, s4, _ = chunk
                    dve.wait_ge(x1_gelu, m + 1)
                    dve.tensor_copy(t3(od[s], ROW)[:, :, D], nw[s][:, 7, 0:ROWS])
                    dve.tensor_tensor(rows_of(od[s]), t3(xd[s4][:, 0:ROWS * D], D), rows_of(od[s]), ALU.add)
                    dve.drain().then_inc(q["made"][s], 1)
                    dve.drain().then_inc(q["free"][s4], 1)

                def step(at):
                    if at(0):
                        scale_shift(at(0))
                    if at(1):
                        add_h(at(1))
                    if at(2):
                        add_x(at(2))
                for s in range(4):
                    dve.sem_inc(q["free"][s], 1)
                for s in range(2):
                    dve.sem_inc(q["sums_free"][s], 1)
                over_chunks(dve, step)

        idx2_staged = sem("idx2_staged")
        gathered2 = [sem(f"gathered2_{s}") for s in range(GROUPS)]
        x1g_free = [sem(f"x1g_free{s}") for s in range(GROUPS)]
        var2_ready = sem("var2_ready")
        std2_ready = sem("std2_ready")
        scale2_ready = sem("scale2_ready")
        h2_ready = sem("h2_ready")
        rows2 = sem("rows2")
        rows2_t = sem("rows2_t")
        run2 = sem("run2")
        carry2 = sem("carry2")
        m_stored = [sem(f"m_stored{j}") for j in range(2)]
        m_blocks = sem("m_blocks")
        out_var = sem("out_var")
        m_blocks_made = sem("m_blocks_made")
        half_landed = [sem(f"half_landed{h}") for h in range(2)]
        half_taken = sem("half_taken")
        out_std = sem("out_std")
        out_scale = sem("out_scale")
        out_h = sem("out_h")
        out_s = sem("out_s")
        s_psum = sem("s_psum")
        sT_ready = sem("sT_ready")
        y_psum = sem("y_psum")
        y_taken = sem("y_taken")
        f = dense_sems("out")
        with nc.Block() as block:
            @block.sync
            def _(sp):
                for h in range(2):
                    load_half(sp, x1t, ROW, 0, h, None, half_landed, half_taken)
                with sp.Fori(0, BLOCKS) as k:
                    for i in range(PIECES_X1):
                        load_halves(sp, k, i, PIECES_X1, x1t, ROW, half_landed, half_taken)
                sp.wait_ge(m_blocks_made, BLOCKS)
                dense_loads(sp, f, x1t, ROW, xd, m_blocks)

            @block.gpsimd
            def _(pool):
                with pool.Fori(0, BLOCKS) as k:
                    for g in range(GROUPS):
                        s = g
                        wait_alone(pool, idx2_staged, k * GROUPS + (g + 1))
                        wait_alone(pool, x1g_free[g], k + 1)
                        for t in range(GROUP):
                            pool.indirect_dma_start(
                                xg[s][:, t * ROW:(t + 1) * ROW], None, x1t,
                                bass.IndirectOffsetOnAxis(ap=idx_stage[s][:, t:t + 1].bitcast(U32), axis=0),
                                bounds_check=N - 1, oob_is_err=False).then_inc(gathered2[s], 16)

                scatter_blocks(pool, m_stored, m_blocks, m_blocks_made)

            @block.scalar
            def _(act):
                def root(k, g):
                    act.wait_ge(var2_ready, k * GROUPS + (g + 1))
                    act.activation(small[g][:, 3, 0:GROUP], small[g][:, 2, 0:GROUP], ACT.Sqrt, bias=eps[:, :],
                                   scale=1.0 / D).then_inc(std2_ready, 1)
                with act.Fori(0, BLOCKS) as k:
                    root(k, 0)
                    for g in range(GROUPS):
                        s, n = g, k * GROUPS + (g + 1)
                        if g + 1 < GROUPS:
                            root(k, g + 1)
                        wait_alone(act, scale2_ready, n)
                        for r in range(GROUP):
                            last = act.activation(rec[:, bass.ds(k * TILES + (g * GROUP + r), 1), 0:D]
                                                  .rearrange("p t c -> p (t c)"), xg[s][:, r * ROW:r * ROW + D], ACT.Relu,
                                                  bias=small[g][:, 5, r:r + 1], scale=small[g][:, 4, r:r + 1])
                        last.then_inc(h2_ready, 1)
                        act.drain().then_inc(x1g_free[s], 1)

                act.wait_ge(m_blocks_made, BLOCKS)
                early = norm_x[:, 0, 0:EARLY * ROWS]
                act.activation(early, early, ACT.Sqrt, bias=eps[:, :], scale=1.0 / D)\
                    .then_inc(out_std, 1)

                def step(at, late):
                    if at(0) and late:
                        m, s = at(0)[0:2]
                        act.wait_ge(out_var, m - (EARLY - 1))
                        act.activation(nw[s][:, 3, 0:ROWS], nw[s][:, 2, 0:ROWS], ACT.Sqrt, bias=eps[:, :],
                                       scale=1.0 / D).then_inc(out_std, 1)
                    if at(0):
                        m, s, u, s4, _ = at(0)
                        act.wait_ge(out_scale, m + 1)
                        if not first_use(u):
                            act.wait_ge(s_psum, m - 1)
                        normalize_rows(act, xd[s4], ROW, s, range(DVE_ROWS, ROWS // 2))
                    if at(1):
                        m = at(1)[0]
                        act.wait_ge(s_psum, m + 1)
                        act.activation(sT, ps_t[:, :], ACT.Copy).then_inc(sT_ready, 1)
                    if at(0):
                        m, s, u, s4, _ = at(0)
                        normalize_rows(act, xd[s4], ROW, s, range(ROWS // 2, ROWS)).then_inc(out_h, 1)
                    if at(2):
                        dense_store(act, f, out, D, at(2))
                over_chunks(act, step, late_from=EARLY)
                for s in range(2):
                    act.wait_ge(f["stored"][s], 16 * ((CHUNKS + 1 - s) // 2))

            @block.tensor
            def _(pe):
                with pe.Fori(0, BLOCKS) as k:
                    wait_alone(pe, rows2, k + 1)
                    for j in range(2):
                        last = pe.transpose(ps_c[0:D, j * P:(j + 1) * P], pk[:, j, 0:D], ident[:, :])
                    last.then_inc(rows2_t, 1)
                    wait_alone(pe, run2, k + 1)
                    pe.transpose(ps_e[:, 0:D], run_v[0:D, 0:P], ident[0:D, 0:D]).then_inc(carry2, 1)

                def step(at):
                    if at(0):
                        m, s, _, _, _ = at(0)
                        wait_alone(pe, out_s, m + 1)
                        for j in range(ROWS // 2):
                            last = pe.transpose(ps_t[:, j * P:(j + 1) * P], hd[s][:, j * P:(j + 1) * P], ident[:, :])
                        last.then_inc(s_psum, 1)
                        pe.wait_ge(y_taken, m + 1)
                        for j in range(ROWS * D // 512):
                            pe.matmul(ps_z[:, j * 512:(j + 1) * 512], ones[:, :], b_rows, start=True, stop=False,
                                      skip_group_check=True)
                        pe.wait_ge(sT_ready, m + 1)
                        for j in range(ROWS // 2):
                            last = pe.matmul(ps_z[:, j * P:(j + 1) * P], sT[:, j * P:(j + 1) * P], w_2[:, :],
                                             start=False, stop=True, skip_group_check=True)
                        last.then_inc(y_psum, 1)
                over_chunks(pe, step)

            @block.vector
            def _(dve):
                dve.memset(run_v[:, :], 0.0)
                for g in range(GROUPS):
                    dve.sem_inc(x1g_free[g], 1)
                    dve.tensor_copy(idx_stage[g][:, 0:GROUP], src_i[:, g * GROUP:(g + 1) * GROUP]).then_inc(idx2_staged, 1)
                for h in range(2):
                    half_sums(dve, 0, h, ROW, half_landed, half_taken)
                def sums(k, g):
                    dve.wait_ge(gathered2[g], (k + 1) * (GROUP * 16))
                    dve.tensor_copy(idx_stage[g][:, 0:GROUP], src_i[:, bass.ds((k + 1) * TILES + g * GROUP, GROUP)])\
                        .then_inc(idx2_staged, 1)
                    for r in range(GROUP):
                        dve.bn_stats(stats[:, r, :], xg[g][:, r * ROW:r * ROW + D])
                    dve.drain()
                    norm_sums(dve, stats, small[g], GROUP).then_inc(var2_ready, 1)

                with dve.Fori(0, BLOCKS) as k:
                    blk = bass.ds(k * TILES, TILES)
                    sums(k, 0)
                    for g in range(GROUPS):
                        s, n = g, k * GROUPS + (g + 1)
                        if g + 1 < GROUPS:
                            sums(k, g + 1)
                        i = g - (GROUPS - PIECES_X1)
                        if i >= 0:
                            half_sums(dve, k * (PIECES_X1 // 2) + (1 + i // 2), i % 2, ROW, half_landed, half_taken)
                        dve.wait_ge(std2_ready, n)
                        rstd, scale, shift = small[g][:, 6, 0:GROUP], small[g][:, 4, 0:GROUP], small[g][:, 5, 0:GROUP]
                        dve.reciprocal(rstd, small[g][:, 3, 0:GROUP])
                        dve.drain()
                        dve.tensor_tensor(scale, rstd, t3(xg[s][:, 0:GROUP * ROW], ROW)[:, :, D], ALU.mult)
                        dve.drain()
                        dve.scalar_tensor_tensor(out=shift, in0=small[g][:, 0, 0:GROUP], scalar=-0.5, in1=scale,
                                                 op0=ALU.mult, op1=ALU.mult).then_inc(scale2_ready, 1)
                    dve.wait_ge(h2_ready, (k + 1) * GROUPS)
                    for c in range(D):
                        col = rec[:, blk, c]
                        dve.tensor_tensor_scan(col, same[:, blk], col, 0.0, ALU.mult, ALU.add)
                    dve.drain()
                    at_end = bass.ds(k * TILES + TILES - 1, 1)
                    dve.tensor_copy(pk[:, 0, 0:D], rec[:, at_end, 0:D].rearrange("p t c -> p (t c)"))
                    dve.tensor_copy(pk[:, 1, 0:D], first[:, at_end].to_broadcast([P, D]))
                    dve.drain().then_inc(rows2, 1)
                    dve.wait_ge(rows2_t, k + 1)
                    scan_over_partitions(dve, row_v, run_v, D, ALU.mult, ALU.add, ps_c).then_inc(run2, 1)
                    dve.wait_ge(carry2, k + 1)
                    dve.tensor_copy(carry[:, 0:D], ps_e[:, 0:D])
                    dve.drain()
                    w3 = t3(wide, D)
                    dve.tensor_tensor(w3, over_c(first[:, blk], D), over_r(carry[:, 0:D], TILES), ALU.mult)
                    dve.drain()
                    dve.tensor_tensor(w3, w3, rec[:, blk, 0:D], ALU.add)
                    dve.drain()
                    dve.tensor_tensor(rec[:, blk, 0:D], w3, over_c(dis_dst[:, blk], D), ALU.mult)
                    dve.drain().then_inc(m_blocks_made, 1)

                dve.wait_ge(out_std, 1)

                def scale_shift(chunk, late):
                    m, s, u, s4, u4 = chunk
                    dis, rstd, inv_deg = t3(xd[s4], ROW)[:, :, D], nw[s][:, 6, 0:ROWS], nw[s][:, 7, 0:ROWS]
                    scale, shift, at = nw[s][:, 4, 0:ROWS], nw[s][:, 5, 0:ROWS], bass.ds(m * ROWS, ROWS)
                    dve.wait_ge(f["landed"][s4], (u4 + 1) * 16)
                    dve.tensor_tensor(inv_deg, dis, dis, ALU.mult)
                    std, mean2 = norm_x[:, 0, at], norm_x[:, 1, at]
                    if late:
                        row_stats(dve, xd[s4], ROW, s).then_inc(out_var, 1)
                        dve.wait_ge(out_std, m - (EARLY - 2))
                        std, mean2 = nw[s][:, 3, 0:ROWS], nw[s][:, 0, 0:ROWS]
                    dve.reciprocal(rstd, std)
                    dve.drain()
                    dve.tensor_tensor(scale, rstd, inv_deg, ALU.mult)
                    dve.drain()
                    dve.scalar_tensor_tensor(out=shift, in0=mean2, scalar=-0.5, in1=scale,
                                             op0=ALU.mult, op1=ALU.mult)
                    dve.drain().then_inc(out_scale, 1)
                    if not first_use(u):
                        dve.wait_ge(s_psum, m - 1)
                    scale_rows(dve, xd[s4], ROW, s, DVE_ROWS)

                def add_sum(chunk):
                    m, s, u, s4, _ = chunk
                    dve.wait_ge(f["sums_landed"][s], (u + 1) * 16)
                    dve.wait_ge(out_h, m + 1)
                    dve.scalar_tensor_tensor(out=t3(hd[s], D), in0=t3(hd[s], D), scalar=0.0, in1=rows_of(ad[s]),
                                             op0=ALU.max, op1=ALU.add).then_inc(out_s, 1)
                    dve.drain().then_inc(f["sums_free"][s], 1)

                def finish(chunk):
                    m, s, u, s4, _ = chunk
                    if not first_use(u):
                        dve.wait_ge(f["stored"][s], u * 16)
                    dve.wait_ge(y_psum, m + 1)
                    dve.tensor_tensor(t3(od[s][:, 0:ROWS * D], D), rows_of(xd[s4]), t3(ps_z[:, :], D), ALU.add)\
                        .then_inc(f["made"][s], 1)
                    dve.drain().then_inc(y_taken, 1)
                    dve.sem_inc(f["free"][s4], 1)

                def step(at, late):
                    if at(0):
                        scale_shift(at(0), late)
                    if at(1):
                        add_sum(at(1))
                    if at(2):
                        finish(at(2))
                for s in range(4):
                    dve.sem_inc(f["free"][s], 1)
                for s in range(2):
                    dve.sem_inc(f["sums_free"][s], 1)
                dve.tensor_copy(t3(b_rows, D), over_r(b2_b[0:1, :], 512 // D))
                dve.drain().then_inc(y_taken, 1)
                over_chunks(dve, step, late_from=EARLY)


_INS = ["x", "src", "dst", "edge_attr_16", "L0_gnn_W_l", "L0_gnn_b_l", "L0_gnn_W_r", "L0_gnn_b_r", "L0_gnn_W_e",
        "L0_gnn_att", "L0_gnn_bias", "L0_gnn_gamma", "L0_gnn_beta", "L1_gnn_W", "L1_gnn_b"]


def kernel(**inputs):
    import numpy as np
    import concourse.bacc as bacc
    from concourse.bass_utils import run_bass_kernel_spmd

    arrays = {name: np.ascontiguousarray(inputs[name]) for name in _INS}
    pad = EP - E
    arrays["src"] = np.concatenate([np.zeros(pad, np.int32), arrays["src"][::-1]])
    arrays["dst"] = np.concatenate([np.full(1, -1, np.int32), np.full(pad, N, np.int32), arrays["dst"][::-1],
                                    np.full(1, -1, np.int32)])
    arrays["edge_attr_16"] = np.concatenate([np.zeros((pad, ED), np.float32), arrays["edge_attr_16"][::-1]])

    nc = bacc.Bacc("TRN2", target_bir_lowering=False, num_devices=1)
    aps = [nc.dram_tensor(f"in_{n}", arrays[n].shape, mybir.dt.from_np(arrays[n].dtype), kind="ExternalInput").ap()
           for n in _INS]
    agg = nc.dram_tensor("agg", (NT, ROW), F32, kind="Internal").ap()
    x1t = nc.dram_tensor("x1t", (N, ROW), F32, kind="Internal").ap()
    out = nc.dram_tensor("out_x", (N, D), F32, kind="ExternalOutput").ap()
    build(nc, *aps, agg, x1t, out)
    r = run_bass_kernel_spmd(nc, [{f"in_{n}": arrays[n] for n in _INS}], core_ids=[0])
    return r.results[0]["out_x"]
```
